# Optimizing a Trainium2 kernel written in Bass

```python
import numpy as np
import jax
import jax.numpy as jnp

def _softmax(x, axis=-1):
    return jax.nn.softmax(x, axis=axis)

def _gelu(x):
    return jax.nn.gelu(x, approximate=True)

def _silu(x):
    return jax.nn.silu(x)

def _sigmoid(x):
    return jax.nn.sigmoid(x)

def _layernorm(x, axis=-1, eps=1e-05):
    m = jnp.mean(x, axis=axis, keepdims=True)
    v = jnp.var(x, axis=axis, keepdims=True)
    return (x - m) / jnp.sqrt(v + eps)

def _scatter_add(tgt, idx, src, axis=0):
    return tgt.at[idx].add(src)

def _segment_sum(src, seg, n):
    return jax.ops.segment_sum(src, seg, n)
kernel_name = 'mk_gnn_resnorm_d1_gnn_r8_62d724'

def setup_inputs(seed: int=0):
    np.random.seed(seed)
    _w = jnp.asarray

    def _rec_inputs():
        import jax
        import jax.numpy as jnp
        _gk = jax.random.key(seed)
        x = -0.0003929 + 0.9999 * jax.random.normal(jax.random.fold_in(_gk, 1), (8192, 256), jnp.float32)
        src = jax.random.randint(jax.random.fold_in(_gk, 2), (131072,), 0, 8192, jnp.int32)
        dst = jax.random.randint(jax.random.fold_in(_gk, 3), (131072,), 0, 8192, jnp.int32)
        _o = jnp.argsort(dst, stable=True)
        src = src[_o]
        dst = dst[_o]
        edge_attr_64 = 8.74812e-05 + 1.00005 * jax.random.normal(jax.random.fold_in(_gk, 12), (131072, 64), jnp.float32)
        return (x, src, dst, edge_attr_64)
    x, src, dst, edge_attr_64 = _rec_inputs()

    def _L0_gnn_setup():
        import math
        import jax, jax.numpy as jnp
        import numpy as np
        N, C, E, ED, B, H = (8192, 256, 131072, 64, 256, 4)
        NPG = N // B
        BN_EPS = 1e-05

        def _bn(h, gamma, beta):
            return h * (gamma / jnp.sqrt(1.0 + BN_EPS)) + beta
        key = jax.random.key(seed)
        ks = jax.random.split(key, 16)
        g = lambda k, shape, fan: (jax.random.normal(k, shape) / np.sqrt(fan)).astype(jnp.float32)
        x = jax.random.normal(ks[0], (N, C), dtype=jnp.float32)
        edge_index = jax.random.randint(ks[1], (2, E), 0, N)
        edge_attr = jax.random.normal(ks[2], (E, ED), dtype=jnp.float32)
        batch = jnp.repeat(jnp.arange(B), NPG)
        return {'x': x, 'edge_attr': edge_attr, 'w_e': g(ks[3], (ED, C), ED), 'b_e': jnp.zeros((C,), jnp.float32), 'w1': g(ks[4], (C, C), C), 'b1': jnp.zeros((C,), jnp.float32), 'w2': g(ks[5], (C, C), C), 'b2': jnp.zeros((C,), jnp.float32), 'bn1_g': jnp.ones((C,), jnp.float32), 'bn1_b': jnp.zeros((C,), jnp.float32), 'in_w': g(ks[6], (3 * C, C), C), 'in_b': jnp.zeros((3 * C,), jnp.float32), 'out_w': g(ks[7], (C, C), C), 'out_b': jnp.zeros((C,), jnp.float32), 'bn2_g': jnp.ones((C,), jnp.float32), 'bn2_b': jnp.zeros((C,), jnp.float32), 'm_w1': g(ks[8], (C, 2 * C), C), 'm_b1': jnp.zeros((2 * C,), jnp.float32), 'm_w2': g(ks[9], (2 * C, C), 2 * C), 'm_b2': jnp.zeros((C,), jnp.float32), 'bn3_g': jnp.ones((C,), jnp.float32), 'bn3_b': jnp.zeros((C,), jnp.float32), 'edge_index': edge_index, 'batch': batch}
    _L0_gnn_all = _L0_gnn_setup()
    _L0_gnn_in = {k: v for k, v in _L0_gnn_all.items() if k in ('w_e', 'b_e', 'w1', 'b1', 'w2', 'b2', 'bn1_g', 'bn1_b', 'in_w', 'in_b', 'out_w', 'out_b', 'bn2_g', 'bn2_b', 'm_w1', 'm_b1', 'm_w2', 'm_b2', 'bn3_g', 'bn3_b')}
    del _L0_gnn_all
    return {'x': x, 'src': src, 'dst': dst, 'edge_attr_64': edge_attr_64, 'L0_gnn_w_e': _L0_gnn_in['w_e'], 'L0_gnn_b_e': _L0_gnn_in['b_e'], 'L0_gnn_w1': _L0_gnn_in['w1'], 'L0_gnn_b1': _L0_gnn_in['b1'], 'L0_gnn_w2': _L0_gnn_in['w2'], 'L0_gnn_b2': _L0_gnn_in['b2'], 'L0_gnn_bn1_g': _L0_gnn_in['bn1_g'], 'L0_gnn_bn1_b': _L0_gnn_in['bn1_b'], 'L0_gnn_in_w': _L0_gnn_in['in_w'], 'L0_gnn_in_b': _L0_gnn_in['in_b'], 'L0_gnn_out_w': _L0_gnn_in['out_w'], 'L0_gnn_out_b': _L0_gnn_in['out_b'], 'L0_gnn_bn2_g': _L0_gnn_in['bn2_g'], 'L0_gnn_bn2_b': _L0_gnn_in['bn2_b'], 'L0_gnn_m_w1': _L0_gnn_in['m_w1'], 'L0_gnn_m_b1': _L0_gnn_in['m_b1'], 'L0_gnn_m_w2': _L0_gnn_in['m_w2'], 'L0_gnn_m_b2': _L0_gnn_in['m_b2'], 'L0_gnn_bn3_g': _L0_gnn_in['bn3_g'], 'L0_gnn_bn3_b': _L0_gnn_in['bn3_b']}

def reference(x, src, dst, edge_attr_64, L0_gnn_w_e, L0_gnn_b_e, L0_gnn_w1, L0_gnn_b1, L0_gnn_w2, L0_gnn_b2, L0_gnn_bn1_g, L0_gnn_bn1_b, L0_gnn_in_w, L0_gnn_in_b, L0_gnn_out_w, L0_gnn_out_b, L0_gnn_bn2_g, L0_gnn_bn2_b, L0_gnn_m_w1, L0_gnn_m_b1, L0_gnn_m_w2, L0_gnn_m_b2, L0_gnn_bn3_g, L0_gnn_bn3_b):
    import jax
    import jax.numpy as jnp

    def _L0_gnn_ref(x, edge_attr, w_e, b_e, w1, b1, w2, b2, bn1_g, bn1_b, in_w, in_b, out_w, out_b, bn2_g, bn2_b, m_w1, m_b1, m_w2, m_b2, bn3_g, bn3_b, edge_index, batch):
        import math
        import jax, jax.numpy as jnp
        import numpy as np
        N, C, E, ED, B, H = (8192, 256, 131072, 64, 256, 4)
        NPG = N // B
        BN_EPS = 1e-05

        def _bn(h, gamma, beta):
            return h * (gamma / jnp.sqrt(1.0 + BN_EPS)) + beta
        src, dst = (edge_index[0], edge_index[1])
        ea = edge_attr @ w_e + b_e
        msg = jax.nn.relu(x[src] + ea)
        agg = jax.ops.segment_sum(msg, dst, num_segments=N)
        t = x + agg
        h_local = jax.nn.relu(t @ w1 + b1) @ w2 + b2
        h_local = _bn(h_local + x, bn1_g, bn1_b)
        hd = x.reshape(B, NPG, C)
        qkv = hd @ in_w.T + in_b
        q, k, v = jnp.split(qkv, 3, axis=-1)
        dh = C // H
        rs = lambda a: a.reshape(B, NPG, H, dh).transpose(0, 2, 1, 3)
        q, k, v = (rs(q), rs(k), rs(v))
        scores = jnp.einsum('bhqd,bhkd->bhqk', q, k) / np.sqrt(dh)
        attn = jax.nn.softmax(scores, axis=-1)
        o = jnp.einsum('bhqk,bhkd->bhqd', attn, v).transpose(0, 2, 1, 3).reshape(B, NPG, C)
        h_attn = (o @ out_w.T + out_b).reshape(N, C)
        h_attn = _bn(h_attn + x, bn2_g, bn2_b)
        out = h_local + h_attn
        out = out + (jax.nn.relu(out @ m_w1 + m_b1) @ m_w2 + m_b2)
        return _bn(out, bn3_g, bn3_b)
    edge_index = jnp.stack([src, dst])
    batch0 = jnp.zeros((8192,), jnp.int32)
    x = _layernorm(x + _L0_gnn_ref(x, edge_attr_64, L0_gnn_w_e, L0_gnn_b_e, L0_gnn_w1, L0_gnn_b1, L0_gnn_w2, L0_gnn_b2, L0_gnn_bn1_g, L0_gnn_bn1_b, L0_gnn_in_w, L0_gnn_in_b, L0_gnn_out_w, L0_gnn_out_b, L0_gnn_bn2_g, L0_gnn_bn2_b, L0_gnn_m_w1, L0_gnn_m_b1, L0_gnn_m_w2, L0_gnn_m_b2, L0_gnn_bn3_g, L0_gnn_bn3_b, edge_index, batch0), axis=-1)
    return x

_drawn_inputs = setup_inputs


def setup_inputs(seed=0):
    import zlib

    import numpy as np

    out = dict(_drawn_inputs(seed))
    spreads = {'L0_gnn_b_e': (0.0, 0.1),
     'L0_gnn_b1': (0.0, 0.724),
     'L0_gnn_b2': (0.0, 0.568),
     'L0_gnn_bn1_g': (1.0, 0.2),
     'L0_gnn_bn1_b': (0.0, 0.624),
     'L0_gnn_in_b': (0.0, 0.464),
     'L0_gnn_out_b': (0.0, 0.577),
     'L0_gnn_bn2_g': (1.0, 0.554),
     'L0_gnn_bn2_b': (0.0, 0.637),
     'L0_gnn_m_b1': (0.0, 0.8),
     'L0_gnn_m_b2': (0.0, 0.697),
     'L0_gnn_bn3_g': (1.0, 0.2),
     'L0_gnn_bn3_b': (0.0, 0.8)}
    factors = {}
    for name, (base, spread) in spreads.items():
        noise = np.random.default_rng([zlib.crc32(name.encode()), seed]).standard_normal(out[name].shape)
        drawn = base * np.exp(spread * noise) if base else spread * noise
        out[name] = jnp.asarray(drawn.astype(out[name].dtype))
    for name, factor in factors.items():
        out[name] = (out[name] * factor).astype(out[name].dtype)
    return out
```

```python
from contextlib import ExitStack

import concourse.bass as bass
from concourse import mybir

fp32 = mybir.dt.float32
f32r = mybir.dt.float32r
i32 = mybir.dt.int32
ALU = mybir.AluOpType
ACT = mybir.ActivationFunctionType
AX = mybir.AxisListType

N, C, E, ED = 8192, 256, 131072, 64
H, NPG = 4, 32
DH = C // H
CC = C // 128
P = 128
TG = 8
GE = TG * P
NG = E // GE
IT = 32
GI = NG // IT
PG = TG // 2
PI = GI * PG
NB = N // IT
CH = 512
NCH = N // CH
BN_SCALE = 1.0 / (1.0 + 1e-5) ** 0.5
LN_EPS = 1e-5
V_INB, V_B1, V_B2, V_G1, V_A1, V_OB, V_G2, V_A2, V_MB1, V_MB2, V_G3, V_A3 = (
    0, 6, 8, 10, 12, 14, 16, 18, 20, 24, 26, 28)
NV = 32


class Kept:
    pass


def gnn_layer(nc, x, src, dst, edge_attr, w_e, b_e, w1, b1, w2, b2, bn1_g, bn1_b, in_w, in_b,
              out_w, out_b, bn2_g, bn2_b, m_w1, m_b1, m_w2, m_b2, bn3_g, bn3_b, out):
    k = Kept()
    k.x, k.src, k.dst, k.edge_attr, k.out = x, src, dst, edge_attr, out
    k.w_e, k.b_e, k.in_w, k.out_w = w_e, b_e, in_w, out_w
    k.w1, k.w2, k.m_w1, k.m_w2 = w1, w2, m_w1, m_w2
    k.vectors = ((in_b, V_INB), (b1, V_B1), (b2, V_B2), (bn1_g, V_G1), (bn1_b, V_A1),
                 (out_b, V_OB), (bn2_g, V_G2), (bn2_b, V_A2), (m_b1, V_MB1), (m_b2, V_MB2),
                 (bn3_g, V_G3), (bn3_b, V_A3))
    k.sum_dram = nc.dram_tensor("sum_dram", (N, C), fp32, kind="Internal").ap()
    k.part_dram = nc.dram_tensor("part_dram", (IT, P, CC, NB), fp32, kind="Internal").ap()

    with ExitStack() as ctx:
        def sb(name, shape, dt=fp32):
            return ctx.enter_context(nc.sbuf_tensor(name, shape, dt))

        k.bank = [ctx.enter_context(nc.psum_tensor(f"bank{n}", [P, 512], fp32)) for n in range(8)]

        k.aggT = sb("aggT", [P, CC, N])
        k.ident = sb("ident", [P, P])
        k.iota = sb("iota", [P, P])
        k.vecT = sb("vecT", [P, NV])
        k.s12 = sb("s12", [P, 8])
        k.c0 = sb("c0", [P, CC])
        k.c3 = sb("c3", [P, CC])
        k.base_i = sb("base_i", [P, P], i32)
        k.bad_i = sb("bad_i", [P, 1], i32)
        k.w1h, k.w1l = sb("w1h", [P, CC, C], f32r), sb("w1l", [P, CC, C], f32r)
        k.w2h, k.w2l = sb("w2h", [P, CC, C], f32r), sb("w2l", [P, CC, C], f32r)
        k.m1h, k.m1l = sb("m1h", [P, CC, 2 * C], f32r), sb("m1l", [P, CC, 2 * C], f32r)
        k.m2h, k.m2l = sb("m2h", [P, 4, C], f32r), sb("m2l", [P, 4, C], f32r)

        with ExitStack() as edge_ctx:
            def eb(name, shape, dt=fp32):
                return edge_ctx.enter_context(nc.sbuf_tensor(name, shape, dt))

            k.rel = eb("rel", [P, NG, TG])
            k.srcs = eb("srcs", [P, NG + 4, TG])
            k.weh, k.wel = eb("weh", [P, C], f32r), eb("wel", [P, C], f32r)
            k.beh = eb("beh", [P, 2 * C], f32r)
            k.ones = eb("ones", [P, P], f32r)
            k.iwh, k.iwl = eb("iwh", [P, CC, 3 * C], f32r), eb("iwl", [P, CC, 3 * C], f32r)
            k.owh, k.owl = eb("owh", [P, CC, C], f32r), eb("owl", [P, CC, C], f32r)
            setup(nc, k)
            edges(nc, k)
            repair(nc, k)
        nodes(nc, k)


class Chain:

    def __init__(self, engine, semaphore):
        self.engine, self.semaphore, self.count = engine, semaphore, 0

    def step(self, instruction):
        instruction.then_inc(self.semaphore, 1)
        self.count += 1

    def settle(self):
        self.engine.wait_ge(self.semaphore, self.count)


def setup(nc, k):
    aggT, ident, vecT, bank = k.aggT, k.ident, k.vecT, k.bank
    with ExitStack() as ctx:
        def sem(name):
            return ctx.enter_context(nc.semaphore(name))

        flat = aggT[:, :, :].rearrange("p c n -> p (c n)")
        used = [0]

        def stage(width):
            used[0] += width
            return flat[:, used[0] - width:used[0]]

        dst_i, src_i = stage(GE).bitcast(i32), stage(GE).bitcast(i32)
        dst_f, src_f, rel_g = stage(GE), stage(GE), stage(GE)
        raw_we = stage(C)
        raw_be = stage(2 * C)
        raw_in = stage(6 * C).rearrange("p (o c) -> p o c", c=C)
        raw_ow = stage(2 * C).rearrange("p (o c) -> p o c", c=C)
        raw_w1 = stage(2 * C).rearrange("p (o c) -> p o c", c=C)
        raw_w2 = stage(2 * C).rearrange("p (o c) -> p o c", c=C)
        raw_m1 = stage(4 * C).rearrange("p (o c) -> p o c", c=2 * C)
        raw_m2 = stage(4 * C).rearrange("p (o c) -> p o c", c=C)
        m2s = stage(4 * C).rearrange("p (o c) -> p o c", c=C)
        be_low = stage(2 * C)
        s3_rows, ones_f = stage(C), stage(P)
        vrows = stage(P)
        lo, hi, base, bad, span = (stage(1) for _ in range(5))
        t0 = stage(2)

        s_dst, s_src, s_we, s_be, s_in, s_ow, s_w, s_vec = (sem(f"s_{n}_loaded") for n in (
            "dst", "src", "we", "be", "in_w", "out_w", "mlp_w", "vec"))
        s_ident, s_clear = sem("s_ident"), sem("s_rows_cleared")
        s_dve = sem("s_dve_chain")
        s_rel, s_base, s_srcf = sem("s_rel_made"), sem("s_base_made"), sem("s_src_cast")
        s_relT, s_srcT, s_baseT, s_vecT = (sem(f"s_{n}_transposed") for n in (
            "rel", "src", "base", "vec"))
        s_inT, s_owT, s_s3T = (sem(f"s_{n}_transposed") for n in ("in_w", "out_w", "s3"))
        s_bank7, s_scales = sem("s_vec_copied"), sem("s_scales_made")
        s_iwh, s_iwl, s_owh = sem("s_iwh"), sem("s_iwl"), sem("s_owh")
        s_m2s, s_m2h = sem("s_m2_scaled"), sem("s_m2h")
        block = ctx.enter_context(nc.Block())

        @block.sync
        def _(sp):
            sp.dma_start(dst_i, k.dst.rearrange("(g e) -> g e", e=GE)).then_inc(s_dst, 16)
            sp.dma_start(src_i, k.src.rearrange("(g e) -> g e", e=GE)).then_inc(s_src, 16)
            for r in range(2):
                sp.dma_start(raw_we[r * ED:(r + 1) * ED, :], k.w_e).then_inc(s_we, 16)
            sp.wait_ge(s_clear, 2)
            for r in range(2):
                for c in range(2):
                    sp.dma_start(raw_be[r:r + 1, c * C:(c + 1) * C],
                                 k.b_e.rearrange("(a n) -> a n", a=1)).then_inc(s_be, 16)
            for v, at in k.vectors:
                rows = v.rearrange("(r c) -> r c", c=P)
                sp.dma_start(vrows[at:at + rows.shape[0], :], rows).then_inc(s_vec, 16)

        @block.gpsimd
        def _(pool):
            nc.gpsimd.memset(ident[:, :], 0.0).then_inc(s_ident, 1)
            pool.wait_ge(s_ident, 1)
            nc.gpsimd.affine_select(out=ident[:, :], in_=ident[:, :], compare_op=ALU.not_equal,
                                    fill=1.0, base=0, pattern=[[-1, P]],
                                    channel_multiplier=1).then_inc(s_ident, 1)
            nc.gpsimd.iota(k.iota[:, :], [[1, P]], base=0, channel_multiplier=0,
                           allow_small_or_imprecise_dtypes=True).then_inc(s_ident, 1)

        @block.vector
        def _(dve):
            own = Chain(dve, s_dve)
            nc.vector.memset(raw_be, 0.0).then_inc(s_clear, 1)
            nc.vector.memset(vrows[0:NV, :], 0.0).then_inc(s_clear, 1)
            nc.vector.memset(k.srcs[:, NG:NG + 4, :], 0.0)
            own.step(nc.vector.memset(ones_f, 1.0))
            own.settle()
            nc.vector.tensor_copy(k.ones[:, :], ones_f)
            dve.wait_ge(s_dst, 16)
            own.step(nc.vector.tensor_copy(dst_f, dst_i))
            own.settle()
            nc.vector.tensor_reduce(hi, dst_f, AX.X, ALU.max)
            own.step(nc.vector.tensor_reduce(lo, dst_f, AX.X, ALU.min))
            own.settle()
            own.step(nc.vector.tensor_scalar(base, lo, float(N - P), None, ALU.min))
            own.settle()
            nc.vector.tensor_scalar(rel_g, dst_f, base, None, ALU.subtract).then_inc(s_rel, 1)
            own.step(nc.vector.tensor_tensor(span, hi, base, ALU.subtract))
            own.settle()
            nc.vector.tensor_scalar(bad, span, float(P - 1), None, ALU.is_gt).then_inc(s_base, 1)
            dve.wait_ge(s_src, 16)
            nc.vector.tensor_copy(src_f, src_i).then_inc(s_srcf, 1)
            dve.wait_ge(s_we, 32)
            own.step(nc.vector.tensor_copy(k.weh[:, :], raw_we))
            own.settle()
            nc.vector.tensor_tensor(k.wel[:, :], raw_we, k.weh[:, :].bitcast(fp32), ALU.subtract)
            dve.wait_ge(s_be, 64)
            own.step(nc.vector.tensor_copy(k.beh[:, :], raw_be))
            own.settle()
            beh = k.beh[:, :].bitcast(fp32)
            own.step(nc.vector.tensor_tensor(be_low, raw_be, beh, ALU.subtract))
            dve.wait_ge(s_ident, 2)
            own.settle()
            own.step(nc.vector.tensor_scalar(be_low, be_low, ident[:, 1:2], None, ALU.mult))
            own.settle()
            nc.vector.scalar_tensor_tensor(k.beh[:, :], beh, ident[:, 0:1], be_low,
                                           ALU.mult, ALU.add)
            for b in range(2):
                dve.wait_ge(s_relT, b + 1)
                nc.vector.tensor_copy(
                    k.rel[:, :, :].rearrange("p g t -> p t g")[:, 4 * b:4 * b + 4, :],
                    bank[b][:, :].rearrange("p (t g) -> p t g", g=NG))
            dve.wait_ge(s_baseT, 1)
            nc.vector.tensor_copy(k.base_i[:, :], bank[7][:, 0:P])
            own.step(nc.vector.tensor_reduce(span, bank[7][:, P:2 * P], AX.X, ALU.max))
            own.settle()
            nc.vector.tensor_copy(k.bad_i[:, :], span).then_inc(s_bank7, 1)
            dve.wait_ge(s_vecT, 1)
            own.step(nc.vector.tensor_copy(vecT[:, :], bank[7][:, 0:NV]))
            own.settle()
            s = k.s12
            for n, v in enumerate((V_G1, V_G2, V_G3)):
                last = nc.vector.tensor_scalar(s[:, 2 * n:2 * n + 2], vecT[:, v:v + 2],
                                               BN_SCALE, None, ALU.mult)
            own.step(last)
            own.settle()
            nc.vector.tensor_tensor(s[:, 6:8], s[:, 0:2], s[:, 2:4], ALU.add).then_inc(s_scales, 1)
            nc.vector.tensor_tensor(k.c0[:, :], s[:, 0:2], vecT[:, V_B2:V_B2 + 2], ALU.mult)
            nc.vector.tensor_tensor(t0, s[:, 2:4], vecT[:, V_OB:V_OB + 2], ALU.mult)
            own.step(nc.vector.tensor_tensor(k.c3[:, :], s[:, 4:6], vecT[:, V_MB2:V_MB2 + 2],
                                             ALU.mult))
            own.settle()
            own.step(nc.vector.tensor_tensor(k.c0[:, :], k.c0[:, :], t0, ALU.add))
            own.settle()
            own.step(nc.vector.tensor_tensor(k.c0[:, :], k.c0[:, :], vecT[:, V_A1:V_A1 + 2],
                                             ALU.add))
            own.settle()
            nc.vector.tensor_tensor(k.c0[:, :], k.c0[:, :], vecT[:, V_A2:V_A2 + 2], ALU.add)
            nc.vector.tensor_tensor(k.c3[:, :], k.c3[:, :], vecT[:, V_A3:V_A3 + 2], ALU.add)
            iwl = k.iwl[:, :, :].rearrange("p c n -> p (c n)")
            iwh = k.iwh[:, :, :].rearrange("p c n -> p (c n)").bitcast(fp32)
            for b in range(3):
                dve.wait_ge(s_iwh, b + 1)
                nc.vector.tensor_tensor(iwl[:, 512 * b:512 * b + 512], bank[4 + b][:, :],
                                        iwh[:, 512 * b:512 * b + 512],
                                        ALU.subtract).then_inc(s_iwl, 1)
            dve.wait_ge(s_owh, 1)
            nc.vector.tensor_tensor(k.owl[:, :, :].rearrange("p c n -> p (c n)"), bank[4][:, :],
                                    k.owh[:, :, :].rearrange("p c n -> p (c n)").bitcast(fp32),
                                    ALU.subtract)
            dve.wait_ge(s_s3T, 1)
            own.step(nc.vector.tensor_copy(s3_rows, bank[5][:, 0:C]))
            own.settle()
            dve.wait_ge(s_w, 64)
            nc.vector.tensor_tensor(m2s, raw_m2, s3_rows.unsqueeze(1).to_broadcast([P, 4, C]),
                                    ALU.mult).then_inc(s_m2s, 1)
            for raw, high, low in ((raw_w1, k.w1h, k.w1l), (raw_w2, k.w2h, k.w2l),
                                   (raw_m1, k.m1h, k.m1l)):
                own.step(nc.vector.tensor_copy(high[:, :, :], raw))
                own.settle()
                own.step(nc.vector.tensor_tensor(low[:, :, :], raw, high[:, :, :].bitcast(fp32),
                                                 ALU.subtract))
            dve.wait_ge(s_m2h, 1)
            own.step(nc.vector.tensor_tensor(k.m2l[:, :, :], m2s, k.m2h[:, :, :].bitcast(fp32),
                                             ALU.subtract))
            own.settle()
            nc.vector.memset(flat, 0.0)

        @block.scalar
        def _(act):
            act.dma_start(raw_in, k.in_w.rearrange("(o p) c -> p o c", p=P)).then_inc(s_in, 16)
            act.dma_start(raw_ow, k.out_w.rearrange("(o p) c -> p o c", p=P)).then_inc(s_ow, 16)
            for raw, w in ((raw_w1, k.w1), (raw_w2, k.w2), (raw_m1, k.m_w1), (raw_m2, k.m_w2)):
                act.dma_start(raw, w.rearrange("(o p) c -> p o c", p=P)).then_inc(s_w, 16)
            for b in range(2):
                act.wait_ge(s_srcT, b + 1)
                nc.scalar.copy(k.srcs[:, 0:NG, :].rearrange("p g t -> p t g")[:, 4 * b:4 * b + 4, :],
                               bank[2 + b][:, :].rearrange("p (t g) -> p t g", g=NG))
            iwh = k.iwh[:, :, :].rearrange("p c n -> p (c n)")
            for b in range(3):
                act.wait_ge(s_inT, b + 1)
                nc.scalar.copy(iwh[:, 512 * b:512 * b + 512], bank[4 + b][:, :]).then_inc(s_iwh, 1)
            act.wait_ge(s_owT, 1)
            nc.scalar.copy(k.owh[:, :, :].rearrange("p c n -> p (c n)"),
                           bank[4][:, :]).then_inc(s_owh, 1)
            act.wait_ge(s_m2s, 1)
            nc.scalar.copy(k.m2h[:, :, :], m2s).then_inc(s_m2h, 1)

        @block.tensor
        def _(pe):
            pe.wait_ge(s_ident, 2)
            for view, made, done, first in ((rel_g, s_rel, s_relT, 0), (src_f, s_srcf, s_srcT, 2)):
                pe.wait_ge(made, 1)
                tiles = view.rearrange("g (p t) -> g t p", t=TG)
                for t in range(TG):
                    ins = nc.tensor.transpose(bank[first + t // 4][:, (t % 4) * P:(t % 4 + 1) * P],
                                              tiles[:, t, :], ident[:, :])
                    if t % 4 == 3:
                        ins.then_inc(done, 1)
            pe.wait_ge(s_base, 1)
            nc.tensor.transpose(bank[7][:, 0:P], base.to_broadcast([P, P]), ident[:, :])
            nc.tensor.transpose(bank[7][:, P:2 * P], bad.to_broadcast([P, P]),
                                ident[:, :]).then_inc(s_baseT, 1)
            pe.wait_ge(s_in, 16)
            for n in range(12):
                cc, o = n // 6, n % 6
                ins = nc.tensor.transpose(bank[4 + n // 4][:, (n % 4) * P:(n % 4 + 1) * P],
                                          raw_in[:, o, cc * P:(cc + 1) * P], ident[:, :])
                if n % 4 == 3:
                    ins.then_inc(s_inT, 1)
            pe.wait_ge(s_vec, 16 * len(k.vectors))
            pe.wait_ge(s_bank7, 1)
            nc.tensor.transpose(bank[7][:, 0:NV], vrows[0:NV, :],
                                ident[0:NV, 0:NV]).then_inc(s_vecT, 1)
            pe.wait_ge(s_ow, 16)
            pe.wait_ge(s_iwl, 1)
            for n in range(4):
                cc, o = n // 2, n % 2
                ins = nc.tensor.transpose(bank[4][:, n * P:(n + 1) * P],
                                          raw_ow[:, o, cc * P:(cc + 1) * P], ident[:, :])
            ins.then_inc(s_owT, 1)
            pe.wait_ge(s_scales, 1)
            pe.wait_ge(s_iwl, 2)
            for c in range(CC):
                ins = nc.tensor.transpose(bank[5][:, c * P:(c + 1) * P],
                                          k.s12[:, 4 + c:5 + c].to_broadcast([P, P]), ident[:, :])
            ins.then_inc(s_s3T, 1)


def edges(nc, k):
    aggT, ident, vecT, bank = k.aggT, k.ident, k.vecT, k.bank
    s_ = k.s12
    EAB = bank[0:4]
    AGB, TRB, AT0, AT1 = bank[4:8]
    with ExitStack() as ctx:
        def sb(name, shape, dt=fp32):
            return ctx.enter_context(nc.sbuf_tensor(name, shape, dt))

        def sem(name):
            return ctx.enter_context(nc.semaphore(name))

        idx = [sb(f"idx{n}", [P, TG], i32) for n in range(4)]
        xg = sb("xg", [P, 8, 2 * C])
        ea = sb("ea", [P, 2, TG, ED])
        eahl = sb("eahl", [P, TG, 2 * ED], f32r)
        eaT = sb("eaT", [P, 2, 4 * P], f32r)
        mh, ml = sb("mh", [P, 4, 2 * C], f32r), sb("ml", [P, 4, 2 * C], f32r)
        onehot = sb("onehot", [P, 2, TG, P], f32r)
        agg = sb("agg", [P, C])
        xn = sb("xn", [P, 2, C])
        xh, xl = sb("xh", [P, CC, NB], f32r), sb("xl", [P, CC, NB], f32r)
        qT, kT = sb("qT", [P, CC, NB]), sb("kT", [P, CC, NB])
        vn = sb("vn", [P, 2, C])
        dif, ex = sb("dif", [P, 2 * H, NPG]), sb("ex", [P, 2 * H, NPG])
        prob, probT = sb("prob", [P, 2 * H, NPG]), sb("probT", [P, 2 * H, NPG])
        mx, sm, rs = sb("mx", [P, 2 * H]), sb("sm", [P, 2 * H]), sb("rs", [P, 2 * H])
        oT = sb("oT", [P, CC, NB])
        oh, ol = sb("oh", [P, CC, NB], f32r), sb("ol", [P, CC, NB], f32r)
        on = sb("on", [P, 2 * C])
        part0, part = sb("part0", [P, CC, NB]), sb("part", [P, CC, NB])

        s_ea = [sem(f"s_edge_attr_{n}") for n in range(2)]
        s_xg = [sem(f"s_gathered_{n}") for n in range(8)]
        s_idx, s_turn, s_scturn = sem("s_idx_copied"), sem("s_gather_turn"), sem("s_score_turn")
        s_eah, s_eal, s_tr, s_eaT = (sem(n) for n in ("s_ea_high", "s_ea_low", "s_ea_transposed",
                                                      "s_eaT_copied"))
        s_prod, s_sum, s_mh, s_ml = (sem(n) for n in ("s_ea_product", "s_x_added", "s_msg_high",
                                                      "s_msg_low"))
        s_hot, s_seg, s_agg, s_aggT, s_added = (sem(n) for n in (
            "s_onehot", "s_pair_summed", "s_agg_copied", "s_agg_transposed", "s_agg_added"))
        s_x, s_xT, s_xh, s_xl = (sem(n) for n in ("s_x_loaded", "s_x_transposed", "s_x_high",
                                                  "s_x_low"))
        s_q, s_qc, s_kk, s_kc, s_v, s_vc = (sem(n) for n in (
            "s_q", "s_q_copied", "s_k", "s_k_copied", "s_v", "s_v_copied"))
        s_sc, s_dif, s_exp, s_prob, s_soft = (sem(n) for n in (
            "s_scores", "s_scores_shifted", "s_exp", "s_probs", "s_softmax_chain"))
        s_o, s_on, s_oT, s_oc, s_oh, s_ol, s_proj = (sem(n) for n in (
            "s_o", "s_o_copied", "s_o_transposed", "s_oT_copied", "s_o_high", "s_o_low", "s_projected"))
        s_part, s_stored = sem("s_part_ready"), sem("s_part_stored")
        block = ctx.enter_context(nc.Block())

        def run(engine, body):
            body(0, True, False)
            with engine.Fori(1, IT - 1) as i:
                body(i, False, False)
            body(IT - 1, False, True)

        src_rows = k.edge_attr.rearrange("(g p t) f -> g p (t f)", p=P, t=TG)
        x_blocks = k.x.rearrange("(i b p) c -> i p b c", b=2, p=P)

        @block.sync
        def _(sp):
            def body(i, first, last):
                for q in range(GI):
                    g = i * GI + q
                    if not (first and q < 2):
                        sp.wait_ge(s_eal, g - 1)
                        sp.wait_ge(s_eah, g - 1)
                    slot = q % 2
                    sp.dma_start(ea[:, slot, :, :].rearrange("p t f -> p (t f)"),
                                 src_rows[bass.ds(g, 1), :, :].rearrange("a p f -> (a p) f")
                                 ).then_inc(s_ea[slot], 16)
                    if q == 0:
                        if not first:
                            sp.wait_ge(s_xT, i)
                        sp.dma_start(xn[:, :, :],
                                     x_blocks[bass.ds(i, 1), :, :, :].rearrange(
                                         "a p b c -> (a p) b c")).then_inc(s_x, 16)
                if not first:
                    sp.wait_ge(s_part, i)
                    sp.dma_start(k.part_dram[bass.ds(i - 1, 1), :, :, :].rearrange(
                        "a p c n -> (a p) c n"), part[:, :, :]).then_inc(s_stored, 16)
            run(sp, body)
            sp.wait_ge(s_part, IT)
            sp.dma_start(k.part_dram[IT - 1, :, :, :], part[:, :, :]).then_inc(s_stored, 16)
            sp.wait_ge(s_stored, 16 * IT)

        @block.gpsimd
        def _(pool):
            def body(i, first, last):
                for q in range(GI):
                    g = i * GI + q
                    for j in range(PG):
                        pair = i * PI + q * PG + j
                        slot = (q * PG + j) % 8
                        if j == 0:
                            pool.wait_ge(s_idx, g + 1)
                        if not (first and q < 2):
                            pool.wait_ge(s_sum, pair - 7)
                        pool.sem_inc(s_turn, 1)
                        for t in range(2):
                            pool.indirect_dma_start(
                                xg[:, slot, t * C:(t + 1) * C], None, k.x[:, :],
                                bass.IndirectOffsetOnAxis(idx[q][:, 2 * j + t:2 * j + t + 1], 0)
                            ).then_inc(s_xg[slot], 16)
            run(pool, body)

        @block.scalar
        def _(act):
            def copy_idx(g, slot):
                nc.scalar.copy(idx[slot][:, :], k.srcs[:, bass.ds(g, 1), :].rearrange(
                    "p a t -> p (a t)")).then_inc(s_idx, 1)

            def split_high(g, slot, uses):
                act.wait_ge(s_ea[slot], 16 * uses)
                nc.scalar.copy(eahl[:, :, 0:ED], ea[:, slot, :, :]).then_inc(s_eah, 1)

            def copy_eaT(half):
                nc.scalar.copy(eaT[:, half, :], TRB[:, :]).then_inc(s_eaT, 1)

            for g in range(3):
                copy_idx(g, g)
            split_high(0, 0, 1)
            act.wait_ge(s_tr, 1)
            copy_eaT(0)

            def body(i, first, last):
                for q in range(GI):
                    g = i * GI + q
                    for j in range(PG):
                        p = q * PG + j
                        pair = i * PI + p
                        if j == 0:
                            if not (last and q == GI - 1):
                                act.wait_ge(s_tr, 2 * g + 2)
                                split_high(g + 1, (q + 1) % 2, 2 * i + (q + 1) // 2 + 1)
                        act.wait_ge(s_sum, pair + 1)
                        if not (first and q == 0):
                            act.wait_ge(s_seg, pair - 3)
                        nc.scalar.activation(mh[:, p % 4, :], EAB[p % 4][:, :],
                                             ACT.Relu).then_inc(s_mh, 1)
                        if j == 0:
                            act.wait_ge(s_tr, 2 * g + 2)
                            if not (first and q == 0):
                                act.wait_ge(s_prod, pair)
                            copy_eaT(1)
                            copy_idx(g + 3, (q + 3) % 4)
                        if j == 1:
                            if not (first and q == 0):
                                act.wait_ge(s_seg, 4 * g)
                                if not (first and q == 1):
                                    act.wait_ge(s_aggT, g - 1)
                                nc.scalar.copy(agg[:, :], AGB[:, 0:C]).then_inc(s_agg, 1)
                            if not (last and q == GI - 1):
                                act.wait_ge(s_tr, 2 * g + 3)
                                act.wait_ge(s_prod, 4 * g + 2)
                                copy_eaT(0)
                        attention(i, p, first)

            def attention(i, p, first):
                if p == 1:
                    act.wait_ge(s_xT, i + 1)
                    if not first:
                        act.wait_ge(s_v, i)
                        act.wait_ge(s_part, i)
                    nc.scalar.copy(xh[:, :, :].rearrange("p c n -> p (c n)"),
                                   AT0[:, :]).then_inc(s_xh, 1)
                    for c in range(CC):
                        ins = nc.scalar.activation(part0[:, c, :], AT0[:, c * NB:(c + 1) * NB],
                                                   ACT.Identity, bias=k.c0[:, c:c + 1],
                                                   scale=s_[:, 6 + c:7 + c])
                    ins.then_inc(s_xh, 1)
                if p in (3, 4):
                    done, to, at, copied, b = ((s_q, qT, AT1, s_qc, 0), (s_kk, kT, AT0, s_kc, 2))[p - 3]
                    act.wait_ge(done, i + 1)
                    if not first:
                        act.wait_ge(s_sc, i)
                    for c in range(CC):
                        ins = nc.scalar.activation(to[:, c, :], at[:, c * NB:(c + 1) * NB],
                                                   ACT.Identity,
                                                   bias=vecT[:, V_INB + b + c:V_INB + b + c + 1])
                    ins.then_inc(copied, 1)
                if p == 6:
                    act.wait_ge(s_v, i + 1)
                    if not first:
                        act.wait_ge(s_o, i)
                    nc.scalar.copy(vn[:, :, :].rearrange("p b c -> p (b c)"),
                                   AT1[:, :]).then_inc(s_vc, 1)
                if p == 8:
                    act.wait_ge(s_dif, i + 1)
                    nc.scalar.activation(ex[:, :, :], dif[:, :, :], ACT.Exp,
                                         scale=DH ** -0.5).then_inc(s_exp, 1)
                if p == 11:
                    act.wait_ge(s_o, i + 1)
                    nc.scalar.copy(on[:, :], AT1[:, :]).then_inc(s_on, 1)
                if p == 13:
                    act.wait_ge(s_oT, i + 1)
                    for c in range(CC):
                        ins = nc.scalar.activation(oT[:, c, :], AT0[:, c * NB:(c + 1) * NB],
                                                   ACT.Identity,
                                                   bias=vecT[:, V_INB + 4 + c:V_INB + 5 + c])
                    ins.then_inc(s_oc, 1)
                    act.wait_ge(s_oc, i + 1)
                    nc.scalar.copy(oh[:, :, :], oT[:, :, :]).then_inc(s_oh, 1)

            run(act, body)
            act.wait_ge(s_seg, 4 * NG)
            act.wait_ge(s_aggT, NG - 1)
            nc.scalar.copy(agg[:, :], AGB[:, 0:C]).then_inc(s_agg, 1)

        @block.vector
        def _(dve):
            def split_low(g, slot):
                dve.wait_ge(s_eah, g + 1)
                nc.vector.tensor_tensor(eahl[:, :, ED:2 * ED], ea[:, slot, :, :],
                                        eahl[:, :, 0:ED].bitcast(fp32),
                                        ALU.subtract).then_inc(s_eal, 1)

            def low_part(pair, slot, first):
                dve.wait_ge(s_mh, pair + 1)
                if not first:
                    dve.wait_ge(s_seg, pair - 3)
                nc.vector.scalar_tensor_tensor(ml[:, slot, :], EAB[slot][:, :], 0.0,
                                               mh[:, slot, :].bitcast(fp32),
                                               ALU.max, ALU.subtract).then_inc(s_ml, 1)

            def add_agg(g):
                at = nc.vector.value_load(k.base_i[0:1, bass.ds(g, 1)], min_val=0, max_val=N - P)
                dve.wait_ge(s_aggT, g + 1)
                if not (isinstance(g, int) and g == 0):
                    dve.wait_ge(s_added, g)
                window = aggT[:, :, bass.ds(at, P)]
                nc.vector.tensor_tensor(window, TRB[:, 0:C].rearrange("p (c n) -> p c n", n=P),
                                        window, ALU.add).then_inc(s_added, 1)

            split_low(0, 0)

            def body(i, first, last):
                for q in range(GI):
                    g = i * GI + q
                    for j in range(PG):
                        p = q * PG + j
                        pair = i * PI + p
                        dve.wait_ge(s_prod, pair + 1)
                        dve.wait_ge(s_xg[p % 8], 32 * (2 * i + p // 8 + 1))
                        nc.vector.tensor_tensor(EAB[p % 4][:, :], EAB[p % 4][:, :],
                                                xg[:, p % 8, :], ALU.add).then_inc(s_sum, 1)
                        if not (first and p == 0):
                            low_part(pair - 1, (p - 1) % 4, first and p < 5)
                        if j == 0 and not (last and q == GI - 1):
                            split_low(g + 1, (q + 1) % 2)
                        if j == 1:
                            if not (first and q < 2):
                                dve.wait_ge(s_seg, 4 * (g - 1))
                            nc.vector.tensor_tensor(
                                onehot[:, q % 2, :, :],
                                k.iota[:, :].unsqueeze(1).to_broadcast([P, TG, P]),
                                k.rel[:, bass.ds(g, 1), :].rearrange("p a t -> p (a t)")
                                .unsqueeze(2).to_broadcast([P, TG, P]),
                                ALU.is_equal).then_inc(s_hot, 1)
                        if j == 3 and not (first and q == 0):
                            add_agg(g - 1)
                        attention(i, p, first)

            def attention(i, p, first):
                if p == 1:
                    dve.wait_ge(s_xh, 2 * i + 2)
                    if not first:
                        dve.wait_ge(s_v, i)
                    nc.vector.tensor_tensor(xl[:, :, :].rearrange("p c n -> p (c n)"), AT0[:, :],
                                            xh[:, :, :].rearrange("p c n -> p (c n)").bitcast(fp32),
                                            ALU.subtract).then_inc(s_xl, 1)
                    nodes_ = aggT[:, :, bass.ds(i * NB, NB)]
                    if not first:
                        dve.wait_ge(s_added, GI * i - 1)
                    nc.vector.tensor_tensor(nodes_, AT0[:, :].rearrange("p (c n) -> p c n", n=NB),
                                            nodes_, ALU.add).then_inc(s_xl, 1)
                if p == 8:
                    dve.wait_ge(s_sc, i + 1)
                    scores = [at[:, 0:H * NPG].rearrange("p (h n) -> p h n", n=NPG)
                              for at in (AT0, AT1)]
                    for n in range(2):
                        ins = nc.vector.tensor_reduce(mx[:, H * n:H * n + H], scores[n],
                                                      AX.X, ALU.max)
                    ins.then_inc(s_soft, 1)
                    dve.wait_ge(s_soft, 4 * i + 1)
                    for n in range(2):
                        ins = nc.vector.tensor_tensor(
                            dif[:, H * n:H * n + H, :], scores[n],
                            mx[:, H * n:H * n + H].unsqueeze(2).to_broadcast([P, H, NPG]),
                            ALU.subtract)
                    ins.then_inc(s_dif, 1)
                if p == 9:
                    dve.wait_ge(s_exp, i + 1)
                    nc.vector.tensor_reduce(sm[:, :], ex[:, :, :], AX.X, ALU.add).then_inc(s_soft, 1)
                    dve.wait_ge(s_soft, 4 * i + 2)
                    nc.vector.reciprocal(rs[:, :], sm[:, :]).then_inc(s_soft, 1)
                    dve.wait_ge(s_soft, 4 * i + 3)
                    nc.vector.tensor_tensor(prob[:, :, :], ex[:, :, :],
                                            rs[:, :].unsqueeze(2).to_broadcast([P, 2 * H, NPG]),
                                            ALU.mult).then_inc(s_soft, 1)
                    dve.wait_ge(s_soft, 4 * i + 4)
                    nc.vector.transpose(probT[:, :, :].rearrange("p h n -> p (h n)"),
                                        prob[:, :, :].rearrange("p h n -> p (h n)")
                                        ).then_inc(s_prob, 1)
                if p == 13:
                    dve.wait_ge(s_oh, i + 1)
                    nc.vector.tensor_tensor(ol[:, :, :], oT[:, :, :], oh[:, :, :].bitcast(fp32),
                                            ALU.subtract).then_inc(s_ol, 1)
                if p == 15:
                    dve.wait_ge(s_proj, i + 1)
                    if not first:
                        dve.wait_ge(s_stored, 16 * i)
                    for c in range(CC):
                        ins = nc.vector.scalar_tensor_tensor(
                            part[:, c, :], AT1[:, c * NB:(c + 1) * NB], s_[:, 2 + c:3 + c],
                            part0[:, c, :], ALU.mult, ALU.add)
                    ins.then_inc(s_part, 1)

            run(dve, body)
            low_part(PI * IT - 1, 3, False)
            add_agg(NG - 1)

        @block.tensor
        def _(pe):
            def transpose_half(half):
                for t in range(4):
                    ins = nc.tensor.transpose(TRB[:, t * P:(t + 1) * P],
                                              eahl[:, 4 * half + t, :].bitcast(fp32), ident[:, :])
                ins.then_inc(s_tr, 1)

            def sum_pair(pair, p, first_of_group, last_of_group):
                q = (p // PG) % GI
                for t in range(2):
                    tile = 2 * (p % PG) + t
                    for m, (part_, start, stop) in enumerate(
                            ((mh, first_of_group and t == 0, False),
                             (ml, False, last_of_group and t == 1))):
                        ins = nc.tensor.matmul(AGB[:, 0:C], onehot[:, q % 2, tile, :],
                                               part_[:, p % 4, t * C:(t + 1) * C],
                                               start=start, stop=stop)
                ins.then_inc(s_seg, 1)

            def transpose_agg():
                for c in range(CC):
                    ins = nc.tensor.transpose(TRB[:, c * P:(c + 1) * P],
                                              agg[:, c * P:(c + 1) * P], ident[:, :])
                ins.then_inc(s_aggT, 1)

            pe.wait_ge(s_eal, 1)
            transpose_half(0)
            pe.wait_ge(s_eaT, 1)
            transpose_half(1)

            def body(i, first, last):
                for q in range(GI):
                    g = i * GI + q
                    for j in range(PG):
                        p = q * PG + j
                        pair = i * PI + p
                        if j % 2 == 0:
                            pe.wait_ge(s_eaT, 2 * g + j // 2 + 1)
                        if not (first and q == 0):
                            pe.wait_ge(s_ml, pair - 3)
                        to = EAB[p % 4]
                        nc.tensor.matmul(to[:, :], k.ones[:, :], k.beh[:, :],
                                         start=True, stop=False)
                        for t in range(2):
                            w = eaT[:, j // 2, ((2 * j + t) % 4) * P:((2 * j + t) % 4 + 1) * P]
                            nc.tensor.matmul(to[:, t * C:(t + 1) * C], w, k.weh[:, :],
                                             start=False, stop=False)
                            ins = nc.tensor.matmul(to[:, t * C:(t + 1) * C], w, k.wel[:, :],
                                                   start=False, stop=t == 1)
                        ins.then_inc(s_prod, 1)
                        if not (first and p < 2):
                            pe.wait_ge(s_ml, pair - 1)
                            if j == 2:
                                pe.wait_ge(s_hot, g + 1)
                                if not (first and q == 0):
                                    pe.wait_ge(s_agg, g)
                            sum_pair(pair - 2, (p - 2) % PI, j == 2, j == 1)
                        if j == 1 and not (last and q == GI - 1):
                            pe.wait_ge(s_eal, g + 2)
                            pe.wait_ge(s_eaT, 2 * g + 2)
                            transpose_half(0)
                        if j == 2 and not (first and q == 0):
                            pe.wait_ge(s_agg, g)
                            if last and q == GI - 1:
                                pe.wait_ge(s_eaT, 2 * g + 2)
                            else:
                                pe.wait_ge(s_eaT, 2 * g + 3)
                            transpose_agg()
                        if j == 3 and not (last and q == GI - 1):
                            if first and q == 0:
                                pe.wait_ge(s_eaT, 2 * g + 3)
                            else:
                                pe.wait_ge(s_added, g)
                            transpose_half(1)
                        attention(i, p, first)

            def split_product(out_, stationary, moving, start_first=True):
                terms = [(c, a, b) for c in range(CC) for a, b in ((0, 0), (0, 1), (1, 0))]
                for n, (c, a, b) in enumerate(terms):
                    ins = nc.tensor.matmul(out_, stationary[a](c), moving[b](c),
                                           start=n == 0, stop=n == len(terms) - 1)
                return ins

            def attention(i, p, first):
                if p == 0:
                    pe.wait_ge(s_x, 16 * (i + 1))
                    if not first:
                        pe.wait_ge(s_oc, i)
                    for c in range(CC):
                        for b in range(2):
                            ins = nc.tensor.transpose(
                                AT0[:, c * NB + b * P:c * NB + (b + 1) * P],
                                xn[:, b, c * P:(c + 1) * P], ident[:, :])
                    ins.then_inc(s_xT, 1)
                if p in (2, 3):
                    to, done, off = ((AT1, s_q, 0), (AT0, s_kk, C))[p - 2]
                    if p == 2:
                        pe.wait_ge(s_xl, 2 * i + 2)
                        if not first:
                            pe.wait_ge(s_part, i)
                    for b in range(2):
                        o = off + b * P
                        ins = split_product(to[:, b * NB:(b + 1) * NB],
                                            [lambda c: k.iwh[:, c, o:o + P],
                                             lambda c: k.iwl[:, c, o:o + P]],
                                            [lambda c: xh[:, c, :], lambda c: xl[:, c, :]])
                    ins.then_inc(done, 1)
                if p == 5:
                    pe.wait_ge(s_qc, i + 1)
                    for b in range(2):
                        ins = split_product(AT1[:, b * C:(b + 1) * C],
                                            [lambda c: xh[:, c, b * P:(b + 1) * P],
                                             lambda c: xl[:, c, b * P:(b + 1) * P]],
                                            [lambda c: k.iwh[:, c, 2 * C:3 * C],
                                             lambda c: k.iwl[:, c, 2 * C:3 * C]])
                    ins.then_inc(s_v, 1)
                if p == 7:
                    pe.wait_ge(s_kc, i + 1)
                    pe.wait_ge(s_vc, i + 1)
                    pe.sem_inc(s_scturn, 1)
                    for b in range(2):
                        for h in range(H):
                            at, c = DH * (h % 2), h // 2
                            col = (2 * b + c) * NPG
                            for n in range(4):
                                o = b * P + n * NPG
                                ins = nc.tensor.matmul(
                                    (AT0, AT1)[h % 2][n * NPG:(n + 1) * NPG, col:col + NPG],
                                    qT[at:at + DH, c, o:o + NPG], kT[at:at + DH, c, o:o + NPG],
                                    start=True, stop=True)
                    ins.then_inc(s_sc, 1)
                if p == 10:
                    pe.wait_ge(s_prob, i + 1)
                    pe.sem_inc(s_scturn, 1)
                    for b in range(2):
                        for h in range(H):
                            for n in range(4):
                                r = slice(n * NPG, (n + 1) * NPG)
                                ins = nc.tensor.matmul(
                                    AT1[r, b * C + h * DH:b * C + (h + 1) * DH],
                                    probT[r, H * (h % 2) + 2 * b + h // 2, :],
                                    vn[r, b, h * DH:(h + 1) * DH], start=True, stop=True)
                    ins.then_inc(s_o, 1)
                if p == 12:
                    pe.wait_ge(s_on, i + 1)
                    for c in range(CC):
                        for b in range(2):
                            ins = nc.tensor.transpose(
                                AT0[:, c * NB + b * P:c * NB + (b + 1) * P],
                                on[:, b * C + c * P:b * C + (c + 1) * P], ident[:, :])
                    ins.then_inc(s_oT, 1)
                if p == 14:
                    pe.wait_ge(s_ol, i + 1)
                    for b in range(CC):
                        ins = split_product(AT1[:, b * NB:(b + 1) * NB],
                                            [lambda c: k.owh[:, c, b * P:(b + 1) * P],
                                             lambda c: k.owl[:, c, b * P:(b + 1) * P]],
                                            [lambda c: oh[:, c, :], lambda c: ol[:, c, :]])
                    ins.then_inc(s_proj, 1)

            run(pe, body)
            for p in (PI - 2, PI - 1):
                pe.wait_ge(s_ml, PI * (IT - 1) + p + 1)
                sum_pair(None, p, False, p == PI - 1)
            pe.wait_ge(s_agg, NG)
            pe.wait_ge(s_added, NG - 1)
            transpose_agg()


def repair(nc, k):
    aggT, ident, bank = k.aggT, k.ident, k.bank
    TILES, BLOCKS = E // P, N // P
    with ExitStack() as ctx:
        def sb(name, shape, dt=fp32):
            return ctx.enter_context(nc.sbuf_tensor(name, shape, dt))

        def sem(name):
            return ctx.enter_context(nc.semaphore(name))

        src_i, dst_i, to_i = sb("src_i", [P, 1], i32), sb("dst_i", [P, 1], i32), sb("to_i", [P, 1], i32)
        dst_f, to_f, earlier = sb("dst_f", [P, 1]), sb("to_f", [P, 1]), sb("earlier", [P, 1])
        feat, featT, we = sb("feat", [P, ED]), sb("featT", [ED, P]), sb("we", [ED, C])
        rows_x, rows_s, msg = sb("rows_x", [P, C]), sb("rows_s", [P, C]), sb("msg", [P, C])
        same, same_low, below = sb("same", [P, P]), sb("same_low", [P, P]), sb("below", [P, P])
        block_rows = sb("block_rows", [P, C])

        s_init, s_load, s_x, s_rows, s_store = (sem(n) for n in (
            "s_init", "s_tile_loaded", "s_x_rows", "s_sum_rows", "s_rows_stored"))
        s_below, s_we, s_dst, s_T, s_featT, s_prod, s_msg, s_sum, s_new, s_chain = (
            sem(n) for n in ("s_below", "s_we", "s_dst_cast", "s_tile_transposed", "s_featT",
                             "s_product", "s_msg", "s_summed", "s_rows_new", "s_repair_chain"))
        s_free = sem("s_tile_free")
        s_turn, s_block, s_blockT, s_placed = (sem(n) for n in (
            "s_repair_turn", "s_block_loaded", "s_block_transposed", "s_block_placed"))
        block = ctx.enter_context(nc.Block())

        def flag(engine):
            return engine.value_load(k.bad_i[0:1, 0:1], min_val=0, max_val=1)

        @block.sync
        def _(sp):
            with sp.If(flag(sp) > 0):
                sp.dma_start(k.sum_dram, k.x).then_inc(s_init, 16)
                with sp.Fori(0, TILES) as t:
                    sp.wait_ge(s_free, t + 1)
                    for to, of in ((src_i, k.src), (dst_i, k.dst)):
                        sp.dma_start(to[:, :], of[bass.ds(t * P, P)].rearrange("(p a) -> p a", a=1)
                                     ).then_inc(s_load, 16)
                    sp.dma_start(feat[:, :], k.edge_attr[bass.ds(t * P, P), :]).then_inc(s_load, 16)
                sp.wait_ge(s_store, 16 * TILES)
                with sp.Fori(0, BLOCKS) as n:
                    sp.wait_ge(s_placed, n + 1)
                    sp.dma_start(block_rows[:, :], k.sum_dram[bass.ds(n * P, P), :]
                                 ).then_inc(s_block, 16)

        @block.gpsimd
        def _(pool):
            with pool.If(flag(pool) > 0):
                nc.gpsimd.memset(below[:, :], 1.0).then_inc(s_below, 1)
                pool.wait_ge(s_below, 1)
                nc.gpsimd.affine_select(out=below[:, :], in_=below[:, :], compare_op=ALU.is_gt,
                                        fill=0.0, base=0, pattern=[[-1, P]],
                                        channel_multiplier=1).then_inc(s_below, 1)
                pool.wait_ge(s_init, 16)
                pool.sem_inc(s_free, 1)
                with pool.Fori(0, TILES) as t:
                    pool.wait_ge(s_load, 48 * t + 48)
                    pool.sem_inc(s_turn, 1)
                    pool.indirect_dma_start(rows_x[:, :], None, k.x[:, :],
                                            bass.IndirectOffsetOnAxis(src_i[:, 0:1], 0)
                                            ).then_inc(s_x, 16)
                    pool.indirect_dma_start(rows_s[:, :], None, k.sum_dram[:, :],
                                            bass.IndirectOffsetOnAxis(dst_i[:, 0:1], 0)
                                            ).then_inc(s_rows, 16)
                    pool.wait_ge(s_new, t + 1)
                    pool.sem_inc(s_turn, 1)
                    pool.indirect_dma_start(k.sum_dram[:, :],
                                            bass.IndirectOffsetOnAxis(to_i[:, 0:1], 0),
                                            rows_s[:, :], None, bounds_check=N - 1,
                                            oob_is_err=False).then_inc(s_store, 16)
                    pool.wait_ge(s_store, 16 * t + 16)
                    pool.sem_inc(s_free, 1)

        @block.scalar
        def _(act):
            with act.If(flag(act) > 0):
                with act.Fori(0, TILES) as t:
                    act.wait_ge(s_T, t + 1)
                    nc.scalar.copy(featT[:, :], bank[0][0:ED, 0:P]).then_inc(s_featT, 1)

        @block.vector
        def _(dve):
            with dve.If(flag(dve) > 0):
                nc.vector.tensor_tensor(we[:, :], k.weh[0:ED, :].bitcast(fp32),
                                        k.wel[0:ED, :].bitcast(fp32), ALU.add).then_inc(s_we, 1)
                dve.wait_ge(s_below, 2)
                with dve.Fori(0, TILES) as t:
                    dve.wait_ge(s_load, 48 * t + 48)
                    dve.sem_inc(s_turn, 1)
                    nc.vector.tensor_copy(dst_f[:, :], dst_i[:, :]).then_inc(s_dst, 1)
                    dve.wait_ge(s_dst, t + 1)
                    dve.wait_ge(s_T, t + 1)
                    nc.vector.tensor_scalar(same[:, :], bank[1][:, 0:P], dst_f[:, 0:1], None,
                                            ALU.is_equal).then_inc(s_chain, 1)
                    dve.wait_ge(s_chain, 4 * t + 1)
                    nc.vector.tensor_tensor(same_low[:, :], same[:, :], below[:, :],
                                            ALU.mult).then_inc(s_chain, 1)
                    dve.wait_ge(s_chain, 4 * t + 2)
                    nc.vector.tensor_reduce(earlier[:, :], same_low[:, :], AX.X,
                                            ALU.max).then_inc(s_chain, 1)
                    dve.wait_ge(s_chain, 4 * t + 3)
                    nc.vector.scalar_tensor_tensor(to_f[:, :], earlier[:, :], float(N), dst_f[:, :],
                                                   ALU.mult, ALU.add).then_inc(s_chain, 1)
                    dve.wait_ge(s_chain, 4 * t + 4)
                    nc.vector.tensor_copy(to_i[:, :], to_f[:, :])
                    dve.wait_ge(s_prod, t + 1)
                    dve.wait_ge(s_x, 16 * t + 16)
                    nc.vector.tensor_tensor(msg[:, :], bank[2][:, 0:C], rows_x[:, :],
                                            ALU.add).then_inc(s_msg, 1)
                    dve.wait_ge(s_msg, 2 * t + 1)
                    nc.vector.tensor_scalar(msg[:, :], msg[:, :], 0.0, None,
                                            ALU.max).then_inc(s_msg, 1)
                    dve.wait_ge(s_sum, t + 1)
                    dve.wait_ge(s_rows, 16 * t + 16)
                    nc.vector.tensor_tensor(rows_s[:, :], bank[3][:, 0:C], rows_s[:, :],
                                            ALU.add).then_inc(s_new, 1)
                dve.sem_inc(s_placed, 1)
                with dve.Fori(0, BLOCKS) as n:
                    dve.wait_ge(s_blockT, n + 1)
                    nc.vector.tensor_copy(aggT[:, :, bass.ds(n * P, P)],
                                          bank[0][:, 0:C].rearrange("p (c n) -> p c n", n=P)
                                          ).then_inc(s_placed, 1)

        @block.tensor
        def _(pe):
            with pe.If(flag(pe) > 0):
                pe.wait_ge(s_we, 1)
                with pe.Fori(0, TILES) as t:
                    pe.wait_ge(s_dst, t + 1)
                    nc.tensor.transpose(bank[1][:, 0:P], dst_f[:, 0:1].to_broadcast([P, P]),
                                        ident[:, :])
                    nc.tensor.transpose(bank[0][0:ED, 0:P], feat[:, :],
                                        ident[:, :]).then_inc(s_T, 1)
                    nc.tensor.matmul(bank[2][:, 0:C], k.ones[:, :], k.beh[:, 0:C],
                                     start=True, stop=False)
                    pe.wait_ge(s_featT, t + 1)
                    nc.tensor.matmul(bank[2][:, 0:C], featT[:, :], we[:, :], start=False,
                                     stop=True).then_inc(s_prod, 1)
                    pe.wait_ge(s_msg, 2 * t + 2)
                    nc.tensor.matmul(bank[3][:, 0:C], same[:, :], msg[:, :], start=True,
                                     stop=True).then_inc(s_sum, 1)
                with pe.Fori(0, BLOCKS) as n:
                    pe.wait_ge(s_block, 16 * n + 16)
                    pe.wait_ge(s_placed, n + 1)
                    for c in range(CC):
                        ins = nc.tensor.transpose(bank[0][:, c * P:(c + 1) * P],
                                                  block_rows[:, c * P:(c + 1) * P], ident[:, :])
                    ins.then_inc(s_blockT, 1)


def nodes(nc, k):
    aggT, ident, vecT, bank = k.aggT, k.ident, k.vecT, k.bank
    s_ = k.s12
    NT = CH // P
    with ExitStack() as ctx:
        def sb(name, shape, dt=fp32):
            return ctx.enter_context(nc.sbuf_tensor(name, shape, dt))

        def sem(name):
            return ctx.enter_context(nc.semaphore(name))

        th, tl = sb("th", [P, CC, CH], f32r), sb("tl", [P, CC, CH], f32r)
        h1 = sb("h1", [P, CC, CH])
        h1h, h1l = sb("h1h", [P, CC, CH], f32r), sb("h1l", [P, CC, CH], f32r)
        part = sb("part2", [P, CC, CH])
        o = sb("o", [P, CC, CH])
        oh, ol = sb("oh2", [P, CC, CH], f32r), sb("ol2", [P, CC, CH], f32r)
        z = sb("z", [P, CC, CH])
        h2 = sb("h2", [P, 2, CH])
        h2h, h2l = sb("h2h", [P, 4, CH], f32r), sb("h2l", [P, 4, CH], f32r)
        xn = sb("xn2", [P, NT, C])
        r, y = sb("r", [P, NT, C]), sb("y", [P, NT, C])
        stats, mv = sb("stats", [P, NT, 6]), sb("mv", [P, NT, 2])
        sd, rstd = sb("sd", [P, NT]), sb("rstd", [P, NT])
        ve, fix = sb("ve", [P, NT]), sb("fix", [P, NT])

        s_part, s_x, s_out = sem("s_part_loaded"), sem("s_x_loaded2"), sem("s_stored")
        s_th, s_tl = sem("s_t_high"), sem("s_t_low")
        s_w1, s_h1h, s_h1l = sem("s_w1"), sem("s_h1_high"), sem("s_h1_low")
        s_w2, s_o, s_z, s_oh, s_ol = (sem(n) for n in ("s_w2", "s_out_made", "s_z", "s_out_high",
                                                       "s_out_low"))
        s_m1, s_h2h, s_h2l = sem("s_m1"), sem("s_h2_high"), sem("s_h2_low")
        s_m2, s_r, s_st, s_mv, s_sd, s_rs, s_y, s_chain = (sem(n) for n in (
            "s_m2", "s_row", "s_stats", "s_variance", "s_deviation", "s_rstd", "s_y",
            "s_norm_chain"))
        s_turn = sem("s_turn")
        block = ctx.enter_context(nc.Block())

        def since(c, first):
            return c >= first if isinstance(c, int) else True

        def run(body):
            def steps(engine):
                for c in range(3):
                    body(engine, c, True, c >= 1, c >= 2)
                with engine.Fori(3, NCH - 1) as c:
                    body(engine, c, True, True, True)
                body(engine, NCH - 1, True, True, True)
                body(engine, NCH, False, True, True)
                body(engine, NCH + 1, False, False, True)
            return steps

        x_v = k.x.rearrange("(c t p) f -> c p t f", t=NT, p=P)
        out_v = k.out.rearrange("(c t p) f -> c p t f", t=NT, p=P)

        @block.sync
        def _(sp):
            def body(sp, c, front, back, norm):
                if front:
                    if since(c, 1):
                        sp.wait_ge(s_o, 2 * c)
                    for two in range(2):
                        sp.dma_start(part[:, :, two * NB:(two + 1) * NB],
                                     k.part_dram[bass.ds(2 * c + two, 1), :, :, :].rearrange(
                                         "a p b n -> (a p) b n")).then_inc(s_part, 16)
                if back:
                    if since(c, 2):
                        sp.wait_ge(s_r, 2 * (c - 1))
                    sp.dma_start(xn[:, :, :], x_v[bass.ds(c - 1, 1), :, :, :].rearrange(
                        "a p t f -> (a p) t f")).then_inc(s_x, 16)
                if norm:
                    sp.wait_ge(s_y, c - 1)
                    sp.dma_start(out_v[bass.ds(c - 2, 1), :, :, :].rearrange(
                        "a p t f -> (a p) t f"), y[:, :, :]).then_inc(s_out, 16)
            run(body)(sp)
            sp.wait_ge(s_out, 16 * NCH)

        @block.scalar
        def _(act):
            def high_of_t(c):
                nc.scalar.copy(th[:, :, :], aggT[:, :, bass.ds(c * CH, CH)]).then_inc(s_th, 1)

            high_of_t(0)

            def body(act, c, front, back, norm):
                if front:
                    for b in range(CC):
                        bias = vecT[:, V_B1 + b:V_B1 + b + 1]
                        act.wait_ge(s_w1, 2 * c + b + 1)
                        if since(c, 1):
                            act.wait_ge(s_h1l, 2 * c)
                            act.wait_ge(s_w2, 2 * c)
                        nc.scalar.activation(h1[:, b, :], bank[b][:, :], ACT.Relu, bias=bias)
                        nc.scalar.activation(h1h[:, b, :], bank[b][:, :], ACT.Relu,
                                             bias=bias).then_inc(s_h1h, 1)
                if norm:
                    act.wait_ge(s_mv, c - 1)
                    nc.scalar.activation(sd[:, :], ve[:, :], ACT.Sqrt).then_inc(s_sd, 1)
                if front and not (isinstance(c, int) and c == NCH - 1):
                    act.wait_ge(s_w1, 2 * c + 2)
                    high_of_t(c + 1)
                if back:
                    for b in range(4):
                        bias = vecT[:, V_MB1 + b:V_MB1 + b + 1]
                        n = 4 * (c - 1) + b
                        act.wait_ge(s_m1, n + 1)
                        if since(c, 2) or b >= 2:
                            act.wait_ge(s_h2l, n - 1)
                        if since(c, 2):
                            act.wait_ge(s_m2, 2 * (c - 1))
                        nc.scalar.activation(h2[:, b % 2, :], bank[2 + b][:, :], ACT.Relu,
                                             bias=bias)
                        nc.scalar.activation(h2h[:, b, :], bank[2 + b][:, :], ACT.Relu,
                                             bias=bias).then_inc(s_h2h, 1)
                if front:
                    for b in range(CC):
                        act.wait_ge(s_o, 2 * c + b + 1)
                        if since(c, 1):
                            act.wait_ge(s_m1, 4 * c)
                        nc.scalar.copy(oh[:, b, :], o[:, b, :]).then_inc(s_oh, 1)
                    if since(c, 1):
                        act.wait_ge(s_m2, 2 * c)
                    for b in range(CC):
                        nc.scalar.activation(z[:, b, :], o[:, b, :], ACT.Identity,
                                             bias=k.c3[:, b:b + 1],
                                             scale=s_[:, 4 + b:5 + b]).then_inc(s_z, 1)
            run(body)(act)

        @block.vector
        def _(dve):
            def low_of_t(c):
                dve.wait_ge(s_th, c + 1)
                nc.vector.tensor_tensor(tl[:, :, :], aggT[:, :, bass.ds(c * CH, CH)],
                                        th[:, :, :].bitcast(fp32), ALU.subtract).then_inc(s_tl, 1)

            low_of_t(0)

            def body(dve, c, front, back, norm):
                if norm:
                    d = c - 2
                    dve.wait_ge(s_x, 16 * (c - 1))
                    for b in range(2):
                        dve.wait_ge(s_m2, 2 * d + b + 1)
                        if since(c, 3):
                            dve.wait_ge(s_y, d)
                        nc.vector.tensor_tensor(
                            r[:, 2 * b:2 * b + 2, :],
                            bank[6 + b][:, :].rearrange("p (t f) -> p t f", f=C),
                            xn[:, 2 * b:2 * b + 2, :], ALU.add).then_inc(s_r, 1)
                        dve.wait_ge(s_r, 2 * d + b + 1)
                        for t in (2 * b, 2 * b + 1):
                            ins = nc.vector.bn_stats(stats[:, t, :], r[:, t, :])
                        ins.then_inc(s_st, 1)
                    dve.wait_ge(s_st, 2 * d + 2)
                    dve.sem_inc(s_turn, 1)
                    for t in range(NT):
                        ins = nc.vector.bn_aggr(mv[:, t, :], stats[:, t, :])
                    ins.then_inc(s_chain, 1)
                    dve.wait_ge(s_chain, 5 * d + 1)
                    nc.vector.tensor_scalar(ve[:, :], mv[:, :, 1], LN_EPS, None,
                                            ALU.add).then_inc(s_mv, 1)
                if front:
                    for b in range(CC):
                        dve.wait_ge(s_h1h, 2 * c + b + 1)
                        nc.vector.tensor_tensor(h1l[:, b, :], h1[:, b, :],
                                                h1h[:, b, :].bitcast(fp32),
                                                ALU.subtract).then_inc(s_h1l, 1)
                if norm:
                    dve.wait_ge(s_sd, c - 1)
                    nc.vector.reciprocal(rstd[:, :], sd[:, :]).then_inc(s_chain, 1)
                    dve.wait_ge(s_chain, 5 * d + 2)
                    nc.vector.tensor_tensor(fix[:, :], rstd[:, :], rstd[:, :],
                                            ALU.mult).then_inc(s_chain, 1)
                    dve.wait_ge(s_chain, 5 * d + 3)
                    nc.vector.tensor_tensor(fix[:, :], fix[:, :], ve[:, :],
                                            ALU.mult).then_inc(s_chain, 1)
                    dve.wait_ge(s_chain, 5 * d + 4)
                    nc.vector.tensor_scalar(fix[:, :], fix[:, :], -0.5, 1.5, ALU.mult,
                                            ALU.add).then_inc(s_chain, 1)
                    dve.wait_ge(s_chain, 5 * d + 5)
                    nc.vector.tensor_tensor(rstd[:, :], rstd[:, :], fix[:, :],
                                            ALU.mult).then_inc(s_rs, 1)
                    dve.wait_ge(s_rs, c - 1)
                    if since(c, 3):
                        dve.wait_ge(s_out, 16 * d)
                    for t in range(NT):
                        ins = nc.vector.tensor_scalar(y[:, t, :], r[:, t, :], mv[:, t, 0:1],
                                                      rstd[:, t:t + 1], ALU.subtract, ALU.mult)
                    ins.then_inc(s_y, 1)
                if front and not (isinstance(c, int) and c == NCH - 1):
                    low_of_t(c + 1)
                if back:
                    for b in range(4):
                        dve.wait_ge(s_h2h, 4 * (c - 1) + b + 1)
                        nc.vector.tensor_tensor(h2l[:, b, :], h2[:, b % 2, :],
                                                h2h[:, b, :].bitcast(fp32),
                                                ALU.subtract).then_inc(s_h2l, 1)
                if front:
                    dve.wait_ge(s_part, 32 * (c + 1))
                    for b in range(CC):
                        dve.wait_ge(s_w2, 2 * c + b + 1)
                        if since(c, 1):
                            dve.wait_ge(s_z, 2 * c)
                        nc.vector.scalar_tensor_tensor(o[:, b, :], bank[b][:, :], s_[:, b:b + 1],
                                                       part[:, b, :], ALU.mult,
                                                       ALU.add).then_inc(s_o, 1)
                    for b in range(CC):
                        dve.wait_ge(s_oh, 2 * c + b + 1)
                        nc.vector.tensor_tensor(ol[:, b, :], o[:, b, :],
                                                oh[:, b, :].bitcast(fp32),
                                                ALU.subtract).then_inc(s_ol, 1)
            run(body)(dve)

        @block.tensor
        def _(pe):
            def product(to, blocks, stationary, moving, more=False):
                terms = [(c, a, b) for c in range(blocks) for a, b in ((0, 0), (0, 1), (1, 0))]
                for n, (c, a, b) in enumerate(terms):
                    ins = nc.tensor.matmul(to, stationary[a](c), moving[b](c), start=n == 0,
                                           stop=not more and n == len(terms) - 1)
                return ins

            def body(pe, c, front, back, norm):
                if front:
                    pe.wait_ge(s_tl, c + 1)
                    if since(c, 1):
                        pe.wait_ge(s_o, 2 * c)
                    for b in range(CC):
                        col = slice(b * P, (b + 1) * P)
                        product(bank[b][:, :], CC,
                                [lambda n: k.w1h[:, n, col], lambda n: k.w1l[:, n, col]],
                                [lambda n: th[:, n, :], lambda n: tl[:, n, :]]).then_inc(s_w1, 1)
                if back:
                    pe.wait_ge(s_ol, 2 * c)
                    for b in range(4):
                        col = slice(b * P, (b + 1) * P)
                        if since(c, 2):
                            pe.wait_ge(s_h2h, 4 * (c - 1))
                        product(bank[2 + b][:, :], CC,
                                [lambda n: k.m1h[:, n, col], lambda n: k.m1l[:, n, col]],
                                [lambda n: oh[:, n, :], lambda n: ol[:, n, :]]).then_inc(s_m1, 1)
                if front:
                    pe.wait_ge(s_h1l, 2 * c + 2)
                    for b in range(CC):
                        col = slice(b * P, (b + 1) * P)
                        product(bank[b][:, :], CC,
                                [lambda n: k.w2h[:, n, col], lambda n: k.w2l[:, n, col]],
                                [lambda n: h1h[:, n, :], lambda n: h1l[:, n, :]]).then_inc(s_w2, 1)
                if back:
                    pe.wait_ge(s_h2l, 4 * c)
                    pe.wait_ge(s_z, 2 * c)
                    if since(c, 2):
                        pe.wait_ge(s_r, 2 * (c - 1))
                    for t in range(NT):
                        row = slice(t * P, (t + 1) * P)
                        to = bank[6 + t // 2][:, (t % 2) * C:(t % 2 + 1) * C]
                        product(to, 4,
                                [lambda n: h2h[:, n, row], lambda n: h2l[:, n, row]],
                                [lambda n: k.m2h[:, n, :], lambda n: k.m2l[:, n, :]], more=True)
                        for n in range(CC):
                            ins = nc.tensor.matmul(to[:, n * P:(n + 1) * P], z[:, n, row],
                                                   ident[:, :], start=False, stop=n == CC - 1)
                        if t % 2:
                            ins.then_inc(s_m2, 1)
            run(body)(pe)


_INS = ["x", "src", "dst", "edge_attr_64"] + ["L0_gnn_" + n for n in (
    "w_e", "b_e", "w1", "b1", "w2", "b2", "bn1_g", "bn1_b", "in_w", "in_b", "out_w", "out_b",
    "bn2_g", "bn2_b", "m_w1", "m_b1", "m_w2", "m_b2", "bn3_g", "bn3_b")]


def kernel(**inputs):
    import numpy as _np
    import concourse.bacc as _bacc
    from concourse import mybir as _mybir
    from concourse.bass_utils import run_bass_kernel_spmd as _run

    nc = _bacc.Bacc("TRN2", target_bir_lowering=False, num_devices=1)
    arrays, args = {}, []
    for name in _INS:
        a = _np.ascontiguousarray(inputs[name])
        arrays[f"in_{name}_dram"] = a
        args.append(nc.dram_tensor(f"in_{name}_dram", a.shape, _mybir.dt.from_np(a.dtype),
                                   kind="ExternalInput").ap())
    out = nc.dram_tensor("out_0_dram", (N, C), fp32, kind="ExternalOutput").ap()
    gnn_layer(nc, *args, out)
    r = _run(nc, [arrays], core_ids=[0])
    return r.results[0]["out_0_dram"]
```

```python
from contextlib import ExitStack

import concourse.bass as bass
from concourse import mybir

fp32 = mybir.dt.float32
f32r = mybir.dt.float32r
i32 = mybir.dt.int32
ALU = mybir.AluOpType
ACT = mybir.ActivationFunctionType
AX = mybir.AxisListType

N, C, E, ED = 8192, 256, 131072, 64
H, NPG = 4, 32
DH = C // H
CC = C // 128
P = 128
TG = 8
GE = TG * P
NG = E // GE
IT = 32
GI = NG // IT
PG = TG // 2
PI = GI * PG
LAG = 3
NB = N // IT
CH = 512
NCH = N // CH
BN_SCALE = 1.0 / (1.0 + 1e-5) ** 0.5
LN_EPS = 1e-5
V_INB, V_B1, V_B2, V_G1, V_A1, V_OB, V_G2, V_A2, V_MB1, V_MB2, V_G3, V_A3 = (
    0, 6, 8, 10, 12, 14, 16, 18, 20, 24, 26, 28)
NV = 32


class Kept:
    pass


def gnn_layer(nc, x, src, dst, edge_attr, w_e, b_e, w1, b1, w2, b2, bn1_g, bn1_b, in_w, in_b,
              out_w, out_b, bn2_g, bn2_b, m_w1, m_b1, m_w2, m_b2, bn3_g, bn3_b, out):
    k = Kept()
    k.x, k.src, k.dst, k.edge_attr, k.out = x, src, dst, edge_attr, out
    k.w_e, k.b_e, k.in_w, k.out_w = w_e, b_e, in_w, out_w
    k.w1, k.w2, k.m_w1, k.m_w2 = w1, w2, m_w1, m_w2
    k.vectors = ((in_b, V_INB), (b1, V_B1), (b2, V_B2), (bn1_g, V_G1), (bn1_b, V_A1),
                 (out_b, V_OB), (bn2_g, V_G2), (bn2_b, V_A2), (m_b1, V_MB1), (m_b2, V_MB2),
                 (bn3_g, V_G3), (bn3_b, V_A3))
    k.sum_dram = nc.dram_tensor("sum_dram", (N, C), fp32, kind="Internal").ap()
    k.xT_dram = nc.dram_tensor("xT_dram", (IT, P, CC, NB), fp32, kind="Internal").ap()
    k.part_dram = nc.dram_tensor("part_dram", (IT, P, CC, NB), fp32, kind="Internal").ap()

    with ExitStack() as ctx:
        def sb(name, shape, dt=fp32):
            return ctx.enter_context(nc.sbuf_tensor(name, shape, dt))

        k.bank = [ctx.enter_context(nc.psum_tensor(f"bank{n}", [P, 512], fp32)) for n in range(8)]

        k.aggT = sb("aggT", [P, CC, N])
        k.ident = sb("ident", [P, P])
        k.iota = sb("iota", [P, P])
        k.vecT = sb("vecT", [P, NV])
        k.s12 = sb("s12", [P, 8])
        k.c0 = sb("c0", [P, CC])
        k.c3 = sb("c3", [P, CC])
        k.base_i = sb("base_i", [P, P], i32)
        k.bad_i = sb("bad_i", [P, 1], i32)
        k.w1h, k.w1l = sb("w1h", [P, CC, C], f32r), sb("w1l", [P, CC, C], f32r)
        k.w2h, k.w2l = sb("w2h", [P, CC, C], f32r), sb("w2l", [P, CC, C], f32r)
        k.m1h, k.m1l = sb("m1h", [P, CC, 2 * C], f32r), sb("m1l", [P, CC, 2 * C], f32r)
        k.m2h, k.m2l = sb("m2h", [P, 4, C], f32r), sb("m2l", [P, 4, C], f32r)

        with ExitStack() as edge_ctx:
            def eb(name, shape, dt=fp32):
                return edge_ctx.enter_context(nc.sbuf_tensor(name, shape, dt))

            k.rel = eb("rel", [P, NG, TG])
            k.srcs = eb("srcs", [P, NG + 4, TG])
            k.weh = eb("weh", [P, C], f32r)
            k.wel = eb("wel", [P, C], f32r)
            k.sel = eb("sel", [P, 1])
            k.iwT = eb("iwT", [P, CC, 3 * C])
            k.owT = eb("owT", [P, CC, C])
            setup(nc, k)
            edges(nc, k)
            repair(nc, k)
        nodes(nc, k)


class Chain:

    def __init__(self, engine, semaphore):
        self.engine, self.semaphore, self.count = engine, semaphore, 0

    def step(self, instruction):
        instruction.then_inc(self.semaphore, 1)
        self.count += 1

    def settle(self):
        self.engine.wait_ge(self.semaphore, self.count)


def setup(nc, k):
    aggT, ident, vecT, bank = k.aggT, k.ident, k.vecT, k.bank
    with ExitStack() as ctx:
        def sem(name):
            return ctx.enter_context(nc.semaphore(name))

        flat = aggT[:, :, :].rearrange("p c n -> p (c n)")
        used = [0]

        def stage(width):
            used[0] += width
            return flat[:, used[0] - width:used[0]]

        dst_i, src_i = stage(GE).bitcast(i32), stage(GE).bitcast(i32)
        dst_f, src_f, rel_g = stage(GE), stage(GE), stage(GE)
        raw_we = stage(C)
        raw_be = stage(C)
        raw_in = stage(6 * C).rearrange("p (o c) -> p o c", c=C)
        raw_ow = stage(2 * C).rearrange("p (o c) -> p o c", c=C)
        raw_w1 = stage(2 * C).rearrange("p (o c) -> p o c", c=C)
        raw_w2 = stage(2 * C).rearrange("p (o c) -> p o c", c=C)
        raw_m1 = stage(4 * C).rearrange("p (o c) -> p o c", c=2 * C)
        raw_m2 = stage(4 * C).rearrange("p (o c) -> p o c", c=C)
        m2s = stage(4 * C).rearrange("p (o c) -> p o c", c=C)
        be_low = stage(C)
        s3_rows = stage(C)
        vrows = stage(P)
        lo, hi, base, bad, span = (stage(1) for _ in range(5))
        t0 = stage(2)

        s_dst, s_src, s_we, s_be, s_in, s_ow, s_w, s_vec = (sem(f"s_{n}_loaded") for n in (
            "dst", "src", "we", "be", "in_w", "out_w", "mlp_w", "vec"))
        s_ident, s_clear = sem("s_ident"), sem("s_rows_cleared")
        s_dve = sem("s_dve_chain")
        s_rel, s_base, s_srcf = sem("s_rel_made"), sem("s_base_made"), sem("s_src_cast")
        s_relT, s_srcT, s_baseT, s_vecT = (sem(f"s_{n}_transposed") for n in (
            "rel", "src", "base", "vec"))
        s_inT, s_owT, s_s3T = (sem(f"s_{n}_transposed") for n in ("in_w", "out_w", "s3"))
        s_bank7, s_scales = sem("s_vec_copied"), sem("s_scales_made")
        s_iw = sem("s_in_w_copied")
        s_m2s, s_m2h = sem("s_m2_scaled"), sem("s_m2h")
        block = ctx.enter_context(nc.Block())

        @block.sync
        def _(sp):
            sp.dma_start(dst_i, k.dst.rearrange("(g e) -> g e", e=GE)).then_inc(s_dst, 16)
            sp.dma_start(src_i, k.src.rearrange("(g e) -> g e", e=GE)).then_inc(s_src, 16)
            for r in range(2):
                sp.dma_start(raw_we[r * ED:(r + 1) * ED, :], k.w_e).then_inc(s_we, 16)
            sp.wait_ge(s_clear, 2)
            for r in range(2):
                sp.dma_start(raw_be[ED + r:ED + r + 1, :],
                             k.b_e.rearrange("(a n) -> a n", a=1)).then_inc(s_be, 16)
            for v, at in k.vectors:
                rows = v.rearrange("(r c) -> r c", c=P)
                sp.dma_start(vrows[at:at + rows.shape[0], :], rows).then_inc(s_vec, 16)

        @block.gpsimd
        def _(pool):
            nc.gpsimd.memset(ident[:, :], 0.0).then_inc(s_ident, 1)
            pool.wait_ge(s_ident, 1)
            nc.gpsimd.affine_select(out=ident[:, :], in_=ident[:, :], compare_op=ALU.not_equal,
                                    fill=1.0, base=0, pattern=[[-1, P]],
                                    channel_multiplier=1).then_inc(s_ident, 1)
            nc.gpsimd.iota(k.iota[:, :], [[1, P]], base=0, channel_multiplier=0,
                           allow_small_or_imprecise_dtypes=True).then_inc(s_ident, 1)

        @block.vector
        def _(dve):
            own = Chain(dve, s_dve)
            nc.vector.memset(raw_be, 0.0).then_inc(s_clear, 1)
            nc.vector.memset(vrows[0:NV, :], 0.0).then_inc(s_clear, 1)
            nc.vector.memset(k.srcs[:, NG:NG + 4, :], 0.0)
            dve.wait_ge(s_dst, 16)
            own.step(nc.vector.tensor_copy(dst_f, dst_i))
            own.settle()
            nc.vector.tensor_reduce(hi, dst_f, AX.X, ALU.max)
            own.step(nc.vector.tensor_reduce(lo, dst_f, AX.X, ALU.min))
            own.settle()
            own.step(nc.vector.tensor_scalar(base, lo, float(N - P), None, ALU.min))
            own.settle()
            nc.vector.tensor_scalar(rel_g, dst_f, base, None, ALU.subtract).then_inc(s_rel, 1)
            own.step(nc.vector.tensor_tensor(span, hi, base, ALU.subtract))
            own.settle()
            nc.vector.tensor_scalar(bad, span, float(P - 1), None, ALU.is_gt).then_inc(s_base, 1)
            dve.wait_ge(s_src, 16)
            nc.vector.tensor_copy(src_f, src_i).then_inc(s_srcf, 1)
            dve.wait_ge(s_we, 32)
            own.step(nc.vector.tensor_copy(k.weh[:, :], raw_we))
            dve.wait_ge(s_be, 32)
            dve.wait_ge(s_ident, 2)
            own.step(nc.vector.tensor_tensor(k.sel[:, :], ident[:, ED:ED + 1],
                                             ident[:, ED + 1:ED + 2], ALU.add))
            own.step(nc.vector.tensor_copy(k.wel[ED:P, :], raw_be[ED:P, :]))
            own.settle()
            nc.vector.tensor_tensor(k.wel[0:ED, :], raw_we[0:ED, :],
                                    k.weh[0:ED, :].bitcast(fp32), ALU.subtract)
            high = k.wel[ED:P, :].bitcast(fp32)
            own.step(nc.vector.tensor_tensor(be_low[ED:P, :], raw_be[ED:P, :], high, ALU.subtract))
            own.settle()
            own.step(nc.vector.tensor_scalar(be_low[ED:P, :], be_low[ED:P, :],
                                             ident[ED:P, ED + 1:ED + 2], None, ALU.mult))
            own.settle()
            nc.vector.scalar_tensor_tensor(k.wel[ED:P, :], high, ident[ED:P, ED:ED + 1],
                                           be_low[ED:P, :], ALU.mult, ALU.add)
            for b in range(2):
                dve.wait_ge(s_relT, b + 1)
                nc.vector.tensor_copy(
                    k.rel[:, :, :].rearrange("p g t -> p t g")[:, 4 * b:4 * b + 4, :],
                    bank[b][:, :].rearrange("p (t g) -> p t g", g=NG))
            dve.wait_ge(s_baseT, 1)
            nc.vector.tensor_copy(k.base_i[:, :], bank[7][:, 0:P])
            own.step(nc.vector.tensor_reduce(span, bank[7][:, P:2 * P], AX.X, ALU.max))
            own.settle()
            nc.vector.tensor_copy(k.bad_i[:, :], span).then_inc(s_bank7, 1)
            dve.wait_ge(s_vecT, 1)
            own.step(nc.vector.tensor_copy(vecT[:, :], bank[7][:, 0:NV]))
            own.settle()
            s = k.s12
            for n, v in enumerate((V_G1, V_G2, V_G3)):
                last = nc.vector.tensor_scalar(s[:, 2 * n:2 * n + 2], vecT[:, v:v + 2],
                                               BN_SCALE, None, ALU.mult)
            own.step(last)
            own.settle()
            nc.vector.tensor_tensor(s[:, 6:8], s[:, 0:2], s[:, 2:4], ALU.add).then_inc(s_scales, 1)
            nc.vector.tensor_tensor(k.c0[:, :], s[:, 0:2], vecT[:, V_B2:V_B2 + 2], ALU.mult)
            nc.vector.tensor_tensor(t0, s[:, 2:4], vecT[:, V_OB:V_OB + 2], ALU.mult)
            own.step(nc.vector.tensor_tensor(k.c3[:, :], s[:, 4:6], vecT[:, V_MB2:V_MB2 + 2],
                                             ALU.mult))
            own.settle()
            own.step(nc.vector.tensor_tensor(k.c0[:, :], k.c0[:, :], t0, ALU.add))
            own.settle()
            own.step(nc.vector.tensor_tensor(k.c0[:, :], k.c0[:, :], vecT[:, V_A1:V_A1 + 2],
                                             ALU.add))
            own.settle()
            nc.vector.tensor_tensor(k.c0[:, :], k.c0[:, :], vecT[:, V_A2:V_A2 + 2], ALU.add)
            nc.vector.tensor_tensor(k.c3[:, :], k.c3[:, :], vecT[:, V_A3:V_A3 + 2], ALU.add)
            dve.wait_ge(s_s3T, 1)
            own.step(nc.vector.tensor_copy(s3_rows, bank[5][:, 0:C]))
            own.settle()
            dve.wait_ge(s_w, 64)
            nc.vector.tensor_tensor(m2s, raw_m2, s3_rows.unsqueeze(1).to_broadcast([P, 4, C]),
                                    ALU.mult).then_inc(s_m2s, 1)
            for raw, high, low in ((raw_w1, k.w1h, k.w1l), (raw_w2, k.w2h, k.w2l),
                                   (raw_m1, k.m1h, k.m1l)):
                own.step(nc.vector.tensor_copy(high[:, :, :], raw))
                own.settle()
                own.step(nc.vector.tensor_tensor(low[:, :, :], raw, high[:, :, :].bitcast(fp32),
                                                 ALU.subtract))
            dve.wait_ge(s_m2h, 1)
            own.step(nc.vector.tensor_tensor(k.m2l[:, :, :], m2s, k.m2h[:, :, :].bitcast(fp32),
                                             ALU.subtract))
            own.settle()
            nc.vector.memset(flat, 0.0)

        @block.scalar
        def _(act):
            act.dma_start(raw_in, k.in_w.rearrange("(o p) c -> p o c", p=P)).then_inc(s_in, 16)
            act.dma_start(raw_ow, k.out_w.rearrange("(o p) c -> p o c", p=P)).then_inc(s_ow, 16)
            for raw, w in ((raw_w1, k.w1), (raw_w2, k.w2), (raw_m1, k.m_w1), (raw_m2, k.m_w2)):
                act.dma_start(raw, w.rearrange("(o p) c -> p o c", p=P)).then_inc(s_w, 16)
            for b in range(2):
                act.wait_ge(s_srcT, b + 1)
                nc.scalar.copy(k.srcs[:, 0:NG, :].rearrange("p g t -> p t g")[:, 4 * b:4 * b + 4, :],
                               bank[2 + b][:, :].rearrange("p (t g) -> p t g", g=NG))
            iwT = k.iwT[:, :, :].rearrange("p c n -> p (c n)")
            for b in range(3):
                act.wait_ge(s_inT, b + 1)
                nc.scalar.copy(iwT[:, 512 * b:512 * b + 512], bank[4 + b][:, :]).then_inc(s_iw, 1)
            act.wait_ge(s_owT, 1)
            nc.scalar.copy(k.owT[:, :, :].rearrange("p c n -> p (c n)"), bank[4][:, :])
            act.wait_ge(s_m2s, 1)
            nc.scalar.copy(k.m2h[:, :, :], m2s).then_inc(s_m2h, 1)

        @block.tensor
        def _(pe):
            pe.wait_ge(s_ident, 2)
            for view, made, done, first in ((rel_g, s_rel, s_relT, 0), (src_f, s_srcf, s_srcT, 2)):
                pe.wait_ge(made, 1)
                tiles = view.rearrange("g (p t) -> g t p", t=TG)
                for t in range(TG):
                    ins = nc.tensor.transpose(bank[first + t // 4][:, (t % 4) * P:(t % 4 + 1) * P],
                                              tiles[:, t, :], ident[:, :])
                    if t % 4 == 3:
                        ins.then_inc(done, 1)
            pe.wait_ge(s_base, 1)
            nc.tensor.transpose(bank[7][:, 0:P], base.to_broadcast([P, P]), ident[:, :])
            nc.tensor.transpose(bank[7][:, P:2 * P], bad.to_broadcast([P, P]),
                                ident[:, :]).then_inc(s_baseT, 1)
            pe.wait_ge(s_in, 16)
            for n in range(12):
                cc, o = n // 6, n % 6
                ins = nc.tensor.transpose(bank[4 + n // 4][:, (n % 4) * P:(n % 4 + 1) * P],
                                          raw_in[:, o, cc * P:(cc + 1) * P], ident[:, :])
                if n % 4 == 3:
                    ins.then_inc(s_inT, 1)
            pe.wait_ge(s_vec, 16 * len(k.vectors))
            pe.wait_ge(s_bank7, 1)
            nc.tensor.transpose(bank[7][:, 0:NV], vrows[0:NV, :],
                                ident[0:NV, 0:NV]).then_inc(s_vecT, 1)
            pe.wait_ge(s_ow, 16)
            pe.wait_ge(s_iw, 1)
            for n in range(4):
                cc, o = n // 2, n % 2
                ins = nc.tensor.transpose(bank[4][:, n * P:(n + 1) * P],
                                          raw_ow[:, o, cc * P:(cc + 1) * P], ident[:, :])
            ins.then_inc(s_owT, 1)
            pe.wait_ge(s_scales, 1)
            pe.wait_ge(s_iw, 2)
            for c in range(CC):
                ins = nc.tensor.transpose(bank[5][:, c * P:(c + 1) * P],
                                          k.s12[:, 4 + c:5 + c].to_broadcast([P, P]), ident[:, :])
            ins.then_inc(s_s3T, 1)


def edges(nc, k):
    aggT, ident, vecT, bank = k.aggT, k.ident, k.vecT, k.bank
    s_ = k.s12
    EAB = bank[0:4]
    AGB, TRB, AT0, AT1 = bank[4:8]
    with ExitStack() as ctx:
        def sb(name, shape, dt=fp32):
            return ctx.enter_context(nc.sbuf_tensor(name, shape, dt))

        def sem(name):
            return ctx.enter_context(nc.semaphore(name))

        idx = [sb(f"idx{n}", [P, TG], i32) for n in range(4)]
        xg = sb("xg", [P, 8, 2 * C])
        ea = sb("ea", [P, 2, TG, ED])
        eahl = sb("eahl", [P, TG, 2 * ED], f32r)
        eaT = sb("eaT", [P, 2, 2, 4 * P], f32r)
        eaT1 = sb("eaT1", [P, 2, 2, 4 * P], f32r)
        mh, ml = sb("mh", [P, 4, 2 * C], f32r), sb("ml", [P, 4, 2 * C], f32r)
        onehot = sb("onehot", [P, 2, TG, P], f32r)
        agg = sb("agg", [P, C])
        xn = sb("xn", [P, 2, C])
        xT = sb("xT", [P, CC, NB])
        qT, kT = sb("qT", [P, CC, NB]), sb("kT", [P, CC, NB])
        vn = sb("vn", [P, 2, C])
        dif, ex = sb("dif", [P, 2 * H, NPG]), sb("ex", [P, 2 * H, NPG])
        prob, probT = sb("prob", [P, 2 * H, NPG]), sb("probT", [P, 2 * H, NPG])
        mx, sm, rs = sb("mx", [P, 2 * H]), sb("sm", [P, 2 * H]), sb("rs", [P, 2 * H])
        oT = sb("oT", [P, CC, NB])
        on = sb("on", [P, 2 * C])
        part = sb("part", [P, CC, NB])

        s_ea = [sem(f"s_edge_attr_{n}") for n in range(2)]
        s_xg = [sem(f"s_gathered_{n}") for n in range(8)]
        s_idx, s_turn, s_scturn = sem("s_idx_copied"), sem("s_gather_turn"), sem("s_score_turn")
        s_eah, s_eal, s_tr, s_eaT = (sem(n) for n in ("s_ea_high", "s_ea_low", "s_ea_transposed",
                                                      "s_eaT_copied"))
        s_prod, s_sum, s_mh, s_ml = (sem(n) for n in ("s_ea_product", "s_x_added", "s_msg_high",
                                                      "s_msg_low"))
        s_hot, s_seg, s_agg, s_aggT, s_added = (sem(n) for n in (
            "s_onehot", "s_pair_summed", "s_agg_copied", "s_agg_transposed", "s_agg_added"))
        s_x, s_xT, s_xc, s_xst = (sem(n) for n in ("s_x_loaded", "s_x_transposed", "s_xT_copied",
                                                   "s_xT_stored"))
        s_q, s_qc, s_kk, s_kc, s_v, s_vc = (sem(n) for n in (
            "s_q", "s_q_copied", "s_k", "s_k_copied", "s_v", "s_v_copied"))
        s_sc, s_dif, s_exp, s_prob, s_soft = (sem(n) for n in (
            "s_scores", "s_scores_shifted", "s_exp", "s_probs", "s_softmax_chain"))
        s_o, s_on, s_oT, s_oc, s_proj = (sem(n) for n in (
            "s_o", "s_o_copied", "s_o_transposed", "s_oT_copied", "s_projected"))
        s_ones = sem("s_ones_set")
        s_part, s_stored = sem("s_part_ready"), sem("s_part_stored")
        block = ctx.enter_context(nc.Block())

        def run(engine, body):
            body(0, True, False)
            with engine.Fori(1, IT - 1) as i:
                body(i, False, False)
            body(IT - 1, False, True)

        src_rows = k.edge_attr.rearrange("(g p t) f -> g p (t f)", p=P, t=TG)
        x_blocks = k.x.rearrange("(i b p) c -> i p b c", b=2, p=P)

        @block.sync
        def _(sp):
            def body(i, first, last):
                for q in range(GI):
                    g = i * GI + q
                    if not (first and q < 2):
                        sp.wait_ge(s_eal, g - 1)
                        sp.wait_ge(s_eah, g - 1)
                    slot = q % 2
                    sp.dma_start(ea[:, slot, :, :].rearrange("p t f -> p (t f)"),
                                 src_rows[bass.ds(g, 1), :, :].rearrange("a p f -> (a p) f")
                                 ).then_inc(s_ea[slot], 16)
                    if q == 0:
                        if not first:
                            sp.wait_ge(s_xT, i)
                        sp.dma_start(xn[:, :, :],
                                     x_blocks[bass.ds(i, 1), :, :, :].rearrange(
                                         "a p b c -> (a p) b c")).then_inc(s_x, 16)
                    if q == 1:
                        sp.wait_ge(s_xc, i + 1)
                        sp.dma_start(k.xT_dram[bass.ds(i, 1), :, :, :].rearrange(
                            "a p c n -> (a p) c n"), xT[:, :, :]).then_inc(s_xst, 16)
                if not first:
                    sp.wait_ge(s_part, i)
                    sp.dma_start(k.part_dram[bass.ds(i - 1, 1), :, :, :].rearrange(
                        "a p c n -> (a p) c n"), part[:, :, :]).then_inc(s_stored, 16)
            run(sp, body)
            sp.wait_ge(s_part, IT)
            sp.dma_start(k.part_dram[IT - 1, :, :, :], part[:, :, :]).then_inc(s_stored, 16)
            sp.wait_ge(s_stored, 16 * IT)
            sp.wait_ge(s_xst, 16 * IT)

        @block.gpsimd
        def _(pool):
            def body(i, first, last):
                for q in range(GI):
                    g = i * GI + q
                    for j in range(PG):
                        pair = i * PI + q * PG + j
                        slot = (q * PG + j) % 8
                        if j == 0:
                            pool.wait_ge(s_idx, g + 1)
                        if not (first and q < 2):
                            pool.wait_ge(s_sum, pair - 7)
                        pool.sem_inc(s_turn, 1)
                        for t in range(2):
                            pool.indirect_dma_start(
                                xg[:, slot, t * C:(t + 1) * C], None, k.x[:, :],
                                bass.IndirectOffsetOnAxis(idx[q][:, 2 * j + t:2 * j + t + 1], 0)
                            ).then_inc(s_xg[slot], 16)
            run(pool, body)

        @block.scalar
        def _(act):
            def copy_idx(g, slot):
                nc.scalar.copy(idx[slot][:, :], k.srcs[:, bass.ds(g, 1), :].rearrange(
                    "p a t -> p (a t)")).then_inc(s_idx, 1)

            def split_high(g, slot, uses):
                act.wait_ge(s_ea[slot], 16 * uses)
                nc.scalar.copy(eahl[:, :, 0:ED], ea[:, slot, :, :]).then_inc(s_eah, 1)

            def copy_eaT(slot, half):
                nc.scalar.copy(eaT[:, slot, half, :], TRB[:, :])
                nc.scalar.copy(eaT1[0:ED, slot, half, :], TRB[0:ED, :]).then_inc(s_eaT, 1)

            def copy_agg(g, unused):
                act.wait_ge(s_seg, 4 * g + 4)
                if not unused:
                    act.wait_ge(s_aggT, g)
                nc.scalar.copy(agg[:, :], AGB[:, 0:C]).then_inc(s_agg, 1)

            for g in range(3):
                copy_idx(g, g)
            split_high(0, 0, 1)
            for half in range(2):
                act.wait_ge(s_tr, half + 1)
                copy_eaT(0, half)

            def body(i, first, last):
                for q in range(GI):
                    g = i * GI + q
                    for j in range(PG):
                        p = q * PG + j
                        pair = i * PI + p
                        if j == 0:
                            if not (last and q == GI - 1):
                                act.wait_ge(s_tr, 2 * g + 2)
                                split_high(g + 1, (q + 1) % 2, 2 * i + (q + 1) // 2 + 1)
                        act.wait_ge(s_sum, pair + 1)
                        if not (first and q == 0):
                            act.wait_ge(s_seg, pair - 3)
                        nc.scalar.activation(mh[:, p % 4, :], EAB[p % 4][:, :],
                                             ACT.Relu).then_inc(s_mh, 1)
                        if j == 0:
                            copy_idx(g + 3, (q + 3) % 4)
                        if j in (1, 2) and not (last and q == GI - 1):
                            act.wait_ge(s_tr, 2 * g + 2 + j)
                            if not (first and q == 0):
                                act.wait_ge(s_prod, 4 * g)
                            copy_eaT((q + 1) % 2, j - 1)
                        if j == 2 and not (first and q == 0):
                            copy_agg(g - 1, first and q == 1)
                        attention(i, p, first)

            def attention(i, p, first):
                if p == 1:
                    act.wait_ge(s_xT, i + 1)
                    if not first:
                        act.wait_ge(s_v, i)
                        act.wait_ge(s_xst, 16 * i)
                    nc.scalar.copy(xT[:, :, :].rearrange("p c n -> p (c n)"),
                                   AT0[:, :]).then_inc(s_xc, 1)
                if p in (3, 4):
                    done, to, at, copied, b = ((s_q, qT, AT1, s_qc, 0), (s_kk, kT, AT0, s_kc, 2))[p - 3]
                    act.wait_ge(done, i + 1)
                    if not first:
                        act.wait_ge(s_sc, i)
                    for c in range(CC):
                        ins = nc.scalar.activation(to[:, c, :], at[:, c * NB:(c + 1) * NB],
                                                   ACT.Identity,
                                                   bias=vecT[:, V_INB + b + c:V_INB + b + c + 1])
                    ins.then_inc(copied, 1)
                if p == 6:
                    act.wait_ge(s_v, i + 1)
                    if not first:
                        act.wait_ge(s_o, i)
                    nc.scalar.copy(vn[:, :, :].rearrange("p b c -> p (b c)"),
                                   AT1[:, :]).then_inc(s_vc, 1)
                if p == 8:
                    act.wait_ge(s_dif, i + 1)
                    nc.scalar.activation(ex[:, :, :], dif[:, :, :], ACT.Exp,
                                         scale=DH ** -0.5).then_inc(s_exp, 1)
                if p == 11:
                    act.wait_ge(s_o, i + 1)
                    nc.scalar.copy(on[:, :], AT1[:, :]).then_inc(s_on, 1)
                if p == 13:
                    act.wait_ge(s_oT, i + 1)
                    for c in range(CC):
                        ins = nc.scalar.activation(oT[:, c, :], AT0[:, c * NB:(c + 1) * NB],
                                                   ACT.Identity,
                                                   bias=vecT[:, V_INB + 4 + c:V_INB + 5 + c])
                    ins.then_inc(s_oc, 1)
                if p == 15:
                    act.wait_ge(s_proj, i + 1)
                    if not first:
                        act.wait_ge(s_stored, 16 * i)
                    for c in range(CC):
                        ins = nc.scalar.activation(part[:, c, :], AT1[:, c * NB:(c + 1) * NB],
                                                   ACT.Identity, bias=k.c0[:, c:c + 1],
                                                   scale=s_[:, 2 + c:3 + c])
                    ins.then_inc(s_part, 1)

            run(act, body)
            copy_agg(NG - 1, False)

        @block.vector
        def _(dve):
            def split_low(g, slot):
                dve.wait_ge(s_eah, g + 1)
                nc.vector.tensor_tensor(eahl[:, :, ED:2 * ED], ea[:, slot, :, :],
                                        eahl[:, :, 0:ED].bitcast(fp32),
                                        ALU.subtract).then_inc(s_eal, 1)

            def low_part(pair, slot, first):
                dve.wait_ge(s_mh, pair + 1)
                if not first:
                    dve.wait_ge(s_seg, pair - 3)
                nc.vector.scalar_tensor_tensor(ml[:, slot, :], EAB[slot][:, :], 0.0,
                                               mh[:, slot, :].bitcast(fp32),
                                               ALU.max, ALU.subtract).then_inc(s_ml, 1)

            def add_agg(g):
                at = nc.vector.value_load(k.base_i[0:1, bass.ds(g, 1)], min_val=0, max_val=N - P)
                dve.wait_ge(s_aggT, g + 1)
                if not (isinstance(g, int) and g == 0):
                    dve.wait_ge(s_added, g)
                window = aggT[:, :, bass.ds(at, P)]
                nc.vector.tensor_tensor(window, TRB[:, 0:C].rearrange("p (c n) -> p c n", n=P),
                                        window, ALU.add).then_inc(s_added, 1)

            for t in (eaT1,):
                nc.vector.tensor_copy(t[ED:P, :, :, :].rearrange("p a b n -> p (a b n)"),
                                      k.sel[ED:P, 0:1].to_broadcast([P - ED, 2 * 2 * 4 * P])
                                      ).then_inc(s_ones, 1)
            split_low(0, 0)

            def body(i, first, last):
                for q in range(GI):
                    g = i * GI + q
                    for j in range(PG):
                        p = q * PG + j
                        pair = i * PI + p
                        dve.wait_ge(s_prod, pair + 1)
                        dve.wait_ge(s_xg[p % 8], 32 * (2 * i + p // 8 + 1))
                        nc.vector.tensor_tensor(EAB[p % 4][:, :], EAB[p % 4][:, :],
                                                xg[:, p % 8, :], ALU.add).then_inc(s_sum, 1)
                        if not (first and p == 0):
                            low_part(pair - 1, (p - 1) % 4, first and p < 5)
                        if j == 0 and not (last and q == GI - 1):
                            split_low(g + 1, (q + 1) % 2)
                        if j == 1:
                            if not (first and q < 2):
                                dve.wait_ge(s_seg, 4 * (g - 1))
                            nc.vector.tensor_tensor(
                                onehot[:, q % 2, :, :],
                                k.iota[:, :].unsqueeze(1).to_broadcast([P, TG, P]),
                                k.rel[:, bass.ds(g, 1), :].rearrange("p a t -> p (a t)")
                                .unsqueeze(2).to_broadcast([P, TG, P]),
                                ALU.is_equal).then_inc(s_hot, 1)
                        if j == 0 and not (first and q < 2):
                            add_agg(g - 2)
                        attention(i, p, first)

            def attention(i, p, first):
                if p == 8:
                    dve.wait_ge(s_sc, i + 1)
                    scores = [at[:, 0:H * NPG].rearrange("p (h n) -> p h n", n=NPG)
                              for at in (AT0, AT1)]
                    for n in range(2):
                        ins = nc.vector.tensor_reduce(mx[:, H * n:H * n + H], scores[n],
                                                      AX.X, ALU.max)
                    ins.then_inc(s_soft, 1)
                    dve.wait_ge(s_soft, 4 * i + 1)
                    for n in range(2):
                        ins = nc.vector.tensor_tensor(
                            dif[:, H * n:H * n + H, :], scores[n],
                            mx[:, H * n:H * n + H].unsqueeze(2).to_broadcast([P, H, NPG]),
                            ALU.subtract)
                    ins.then_inc(s_dif, 1)
                if p == 9:
                    dve.wait_ge(s_exp, i + 1)
                    nc.vector.tensor_reduce(sm[:, :], ex[:, :, :], AX.X, ALU.add).then_inc(s_soft, 1)
                    dve.wait_ge(s_soft, 4 * i + 2)
                    nc.vector.reciprocal(rs[:, :], sm[:, :]).then_inc(s_soft, 1)
                    dve.wait_ge(s_soft, 4 * i + 3)
                    nc.vector.tensor_tensor(prob[:, :, :], ex[:, :, :],
                                            rs[:, :].unsqueeze(2).to_broadcast([P, 2 * H, NPG]),
                                            ALU.mult).then_inc(s_soft, 1)
                    dve.wait_ge(s_soft, 4 * i + 4)
                    nc.vector.transpose(probT[:, :, :].rearrange("p h n -> p (h n)"),
                                        prob[:, :, :].rearrange("p h n -> p (h n)")
                                        ).then_inc(s_prob, 1)

            run(dve, body)
            low_part(PI * IT - 1, 3, False)
            add_agg(NG - 2)
            add_agg(NG - 1)

        @block.tensor
        def _(pe):
            def transpose_half(half):
                for t in range(4):
                    ins = nc.tensor.transpose(TRB[:, t * P:(t + 1) * P],
                                              eahl[:, 4 * half + t, :].bitcast(fp32), ident[:, :])
                ins.then_inc(s_tr, 1)

            def sum_pair(p):
                q, j = p // PG, p % PG
                for t in range(2):
                    for half in (mh, ml):
                        ins = nc.tensor.matmul(AGB[:, 0:C], onehot[:, q % 2, 2 * j + t, :],
                                               half[:, p % 4, t * C:(t + 1) * C],
                                               start=j == 0 and t == 0 and half is mh,
                                               stop=j == PG - 1 and t == 1 and half is ml)
                ins.then_inc(s_seg, 1)

            def transpose_agg():
                for c in range(CC):
                    ins = nc.tensor.transpose(TRB[:, c * P:(c + 1) * P],
                                              agg[:, c * P:(c + 1) * P], ident[:, :])
                ins.then_inc(s_aggT, 1)

            pe.wait_ge(s_eal, 1)
            transpose_half(0)
            pe.wait_ge(s_eaT, 1)
            transpose_half(1)
            pe.wait_ge(s_ones, 1)

            def body(i, first, last):
                for q in range(GI):
                    g = i * GI + q
                    for j in range(PG):
                        p = q * PG + j
                        pair = i * PI + p
                        if j % 2 == 0:
                            pe.wait_ge(s_eaT, 2 * g + j // 2 + 1)
                        if not (first and q == 0):
                            pe.wait_ge(s_ml, pair - 3)
                        for t in range(2):
                            to = EAB[p % 4][:, t * C:(t + 1) * C]
                            cols = slice((2 * j + t) % 4 * P, ((2 * j + t) % 4 + 1) * P)
                            nc.tensor.matmul(to, eaT[:, q % 2, j // 2, cols], k.weh[:, :],
                                             start=True, stop=False)
                            ins = nc.tensor.matmul(to, eaT1[:, q % 2, j // 2, cols], k.wel[:, :],
                                                   start=False, stop=True)
                        ins.then_inc(s_prod, 1)
                        if not (first and p < LAG):
                            pe.wait_ge(s_ml, pair - LAG + 1)
                            if j == LAG % PG:
                                pe.wait_ge(s_hot, g + 1)
                                if not (first and q == 0):
                                    pe.wait_ge(s_agg, g)
                            sum_pair((p - LAG) % PI)
                        if j in (1, 2) and not (last and q == GI - 1):
                            if j == 1:
                                pe.wait_ge(s_eal, g + 2)
                                if not (first and q < 2):
                                    pe.wait_ge(s_added, g - 1)
                            pe.wait_ge(s_eaT, 2 * g + 1 + j)
                            transpose_half(j - 1)
                        if j == 3 and not (first and q == 0):
                            pe.wait_ge(s_agg, g)
                            pe.wait_ge(s_eaT, 2 * g + (2 if last and q == GI - 1 else 4))
                            if last and q == GI - 1:
                                pe.wait_ge(s_added, g - 1)
                            transpose_agg()
                        attention(i, p, first)

            def product(to, stationary, moving):
                for c in range(CC):
                    ins = nc.tensor.matmul(to, stationary(c), moving(c), start=c == 0,
                                           stop=c == CC - 1)
                return ins

            def attention(i, p, first):
                if p == 0:
                    pe.wait_ge(s_x, 16 * (i + 1))
                    if not first:
                        pe.wait_ge(s_oc, i)
                    for c in range(CC):
                        for b in range(2):
                            ins = nc.tensor.transpose(
                                AT0[:, c * NB + b * P:c * NB + (b + 1) * P],
                                xn[:, b, c * P:(c + 1) * P], ident[:, :])
                    ins.then_inc(s_xT, 1)
                if p in (2, 3):
                    to, done, off = ((AT1, s_q, 0), (AT0, s_kk, C))[p - 2]
                    if p == 2:
                        pe.wait_ge(s_xc, i + 1)
                        if not first:
                            pe.wait_ge(s_part, i)
                    for b in range(2):
                        o = off + b * P
                        ins = product(to[:, b * NB:(b + 1) * NB],
                                      lambda c: k.iwT[:, c, o:o + P], lambda c: xT[:, c, :])
                    ins.then_inc(done, 1)
                if p == 5:
                    pe.wait_ge(s_qc, i + 1)
                    for b in range(2):
                        ins = product(AT1[:, b * C:(b + 1) * C],
                                      lambda c: xT[:, c, b * P:(b + 1) * P],
                                      lambda c: k.iwT[:, c, 2 * C:3 * C])
                    ins.then_inc(s_v, 1)
                if p == 7:
                    pe.wait_ge(s_kc, i + 1)
                    pe.wait_ge(s_vc, i + 1)
                    pe.sem_inc(s_scturn, 1)
                    for b in range(2):
                        for h in range(H):
                            at, c = DH * (h % 2), h // 2
                            col = (2 * b + c) * NPG
                            for n in range(4):
                                o = b * P + n * NPG
                                ins = nc.tensor.matmul(
                                    (AT0, AT1)[h % 2][n * NPG:(n + 1) * NPG, col:col + NPG],
                                    qT[at:at + DH, c, o:o + NPG], kT[at:at + DH, c, o:o + NPG],
                                    start=True, stop=True)
                    ins.then_inc(s_sc, 1)
                if p == 10:
                    pe.wait_ge(s_prob, i + 1)
                    pe.sem_inc(s_scturn, 1)
                    for b in range(2):
                        for h in range(H):
                            for n in range(4):
                                r = slice(n * NPG, (n + 1) * NPG)
                                ins = nc.tensor.matmul(
                                    AT1[r, b * C + h * DH:b * C + (h + 1) * DH],
                                    probT[r, H * (h % 2) + 2 * b + h // 2, :],
                                    vn[r, b, h * DH:(h + 1) * DH], start=True, stop=True)
                    ins.then_inc(s_o, 1)
                if p == 12:
                    pe.wait_ge(s_on, i + 1)
                    for c in range(CC):
                        for b in range(2):
                            ins = nc.tensor.transpose(
                                AT0[:, c * NB + b * P:c * NB + (b + 1) * P],
                                on[:, b * C + c * P:b * C + (c + 1) * P], ident[:, :])
                    ins.then_inc(s_oT, 1)
                if p == 14:
                    pe.wait_ge(s_oc, i + 1)
                    for b in range(CC):
                        ins = product(AT1[:, b * NB:(b + 1) * NB],
                                      lambda c: k.owT[:, c, b * P:(b + 1) * P],
                                      lambda c: oT[:, c, :])
                    ins.then_inc(s_proj, 1)

            run(pe, body)
            for p in range(PI - LAG, PI):
                pe.wait_ge(s_ml, PI * (IT - 1) + p + 1)
                sum_pair(p)
            pe.wait_ge(s_agg, NG)
            pe.wait_ge(s_added, NG - 1)
            transpose_agg()


def repair(nc, k):
    aggT, ident, bank = k.aggT, k.ident, k.bank
    TILES, BLOCKS = E // P, N // P
    with ExitStack() as ctx:
        def sb(name, shape, dt=fp32):
            return ctx.enter_context(nc.sbuf_tensor(name, shape, dt))

        def sem(name):
            return ctx.enter_context(nc.semaphore(name))

        src_i, dst_i, to_i = sb("src_i", [P, 1], i32), sb("dst_i", [P, 1], i32), sb("to_i", [P, 1], i32)
        dst_f, to_f, earlier = sb("dst_f", [P, 1]), sb("to_f", [P, 1]), sb("earlier", [P, 1])
        feat, featT, we = sb("feat", [P, ED]), sb("featT", [P, P]), sb("we", [P, C])
        rows_x, rows_s, msg = sb("rows_x", [P, C]), sb("rows_s", [P, C]), sb("msg", [P, C])
        same, same_low, below = sb("same", [P, P]), sb("same_low", [P, P]), sb("below", [P, P])
        block_rows = sb("block_rows", [P, C])

        s_init, s_load, s_x, s_rows, s_store = (sem(n) for n in (
            "s_init", "s_tile_loaded", "s_x_rows", "s_sum_rows", "s_rows_stored"))
        s_below, s_we, s_dst, s_T, s_featT, s_prod, s_msg, s_sum, s_new, s_chain = (
            sem(n) for n in ("s_below", "s_we", "s_dst_cast", "s_tile_transposed", "s_featT",
                             "s_product", "s_msg", "s_summed", "s_rows_new", "s_repair_chain"))
        s_free, s_zero = sem("s_tile_free"), sem("s_zeroed")
        s_turn, s_block, s_blockT, s_placed = (sem(n) for n in (
            "s_repair_turn", "s_block_loaded", "s_block_transposed", "s_block_placed"))
        block = ctx.enter_context(nc.Block())

        def flag(engine):
            return engine.value_load(k.bad_i[0:1, 0:1], min_val=0, max_val=1)

        @block.sync
        def _(sp):
            with sp.If(flag(sp) > 0):
                for n in range(CC):
                    sp.wait_ge(s_zero, 1)
                    sp.dma_start(k.sum_dram.rearrange("(n p r) c -> n p (r c)", n=CC, p=P)[n, :, :],
                                 aggT[:, n, :]).then_inc(s_init, 16)
                with sp.Fori(0, TILES) as t:
                    sp.wait_ge(s_free, t + 1)
                    for to, of in ((src_i, k.src), (dst_i, k.dst)):
                        sp.dma_start(to[:, :], of[bass.ds(t * P, P)].rearrange("(p a) -> p a", a=1)
                                     ).then_inc(s_load, 16)
                    sp.dma_start(feat[:, :], k.edge_attr[bass.ds(t * P, P), :]).then_inc(s_load, 16)
                sp.wait_ge(s_store, 16 * TILES)
                with sp.Fori(0, BLOCKS) as n:
                    sp.wait_ge(s_placed, n + 1)
                    sp.dma_start(block_rows[:, :], k.sum_dram[bass.ds(n * P, P), :]
                                 ).then_inc(s_block, 16)

        @block.gpsimd
        def _(pool):
            with pool.If(flag(pool) > 0):
                nc.gpsimd.memset(below[:, :], 1.0).then_inc(s_below, 1)
                pool.wait_ge(s_below, 1)
                nc.gpsimd.affine_select(out=below[:, :], in_=below[:, :], compare_op=ALU.is_gt,
                                        fill=0.0, base=0, pattern=[[-1, P]],
                                        channel_multiplier=1).then_inc(s_below, 1)
                pool.wait_ge(s_init, 16 * CC)
                pool.sem_inc(s_free, 1)
                with pool.Fori(0, TILES) as t:
                    pool.wait_ge(s_load, 48 * t + 48)
                    pool.sem_inc(s_turn, 1)
                    pool.indirect_dma_start(rows_x[:, :], None, k.x[:, :],
                                            bass.IndirectOffsetOnAxis(src_i[:, 0:1], 0)
                                            ).then_inc(s_x, 16)
                    pool.indirect_dma_start(rows_s[:, :], None, k.sum_dram[:, :],
                                            bass.IndirectOffsetOnAxis(dst_i[:, 0:1], 0)
                                            ).then_inc(s_rows, 16)
                    pool.wait_ge(s_new, t + 1)
                    pool.sem_inc(s_turn, 1)
                    pool.indirect_dma_start(k.sum_dram[:, :],
                                            bass.IndirectOffsetOnAxis(to_i[:, 0:1], 0),
                                            rows_s[:, :], None, bounds_check=N - 1,
                                            oob_is_err=False).then_inc(s_store, 16)
                    pool.wait_ge(s_store, 16 * t + 16)
                    pool.sem_inc(s_free, 1)

        @block.scalar
        def _(act):
            with act.If(flag(act) > 0):
                with act.Fori(0, TILES) as t:
                    act.wait_ge(s_T, t + 1)
                    nc.scalar.copy(featT[0:ED, :], bank[0][0:ED, 0:P]).then_inc(s_featT, 1)

        @block.vector
        def _(dve):
            with dve.If(flag(dve) > 0):
                nc.vector.memset(aggT[:, :, :].rearrange("p c n -> p (c n)"), 0.0
                                 ).then_inc(s_zero, 1)
                nc.vector.tensor_copy(we[ED:P, :], k.wel[ED:P, :].bitcast(fp32))
                nc.vector.tensor_copy(featT[ED:P, :], k.sel[ED:P, 0:1].to_broadcast([P - ED, P]))
                nc.vector.tensor_tensor(we[0:ED, :], k.weh[0:ED, :].bitcast(fp32),
                                        k.wel[0:ED, :].bitcast(fp32), ALU.add).then_inc(s_we, 1)
                dve.wait_ge(s_below, 2)
                with dve.Fori(0, TILES) as t:
                    dve.wait_ge(s_load, 48 * t + 48)
                    dve.sem_inc(s_turn, 1)
                    nc.vector.tensor_copy(dst_f[:, :], dst_i[:, :]).then_inc(s_dst, 1)
                    dve.wait_ge(s_dst, t + 1)
                    dve.wait_ge(s_T, t + 1)
                    nc.vector.tensor_scalar(same[:, :], bank[1][:, 0:P], dst_f[:, 0:1], None,
                                            ALU.is_equal).then_inc(s_chain, 1)
                    dve.wait_ge(s_chain, 4 * t + 1)
                    nc.vector.tensor_tensor(same_low[:, :], same[:, :], below[:, :],
                                            ALU.mult).then_inc(s_chain, 1)
                    dve.wait_ge(s_chain, 4 * t + 2)
                    nc.vector.tensor_reduce(earlier[:, :], same_low[:, :], AX.X,
                                            ALU.max).then_inc(s_chain, 1)
                    dve.wait_ge(s_chain, 4 * t + 3)
                    nc.vector.scalar_tensor_tensor(to_f[:, :], earlier[:, :], float(N), dst_f[:, :],
                                                   ALU.mult, ALU.add).then_inc(s_chain, 1)
                    dve.wait_ge(s_chain, 4 * t + 4)
                    nc.vector.tensor_copy(to_i[:, :], to_f[:, :])
                    dve.wait_ge(s_prod, t + 1)
                    dve.wait_ge(s_x, 16 * t + 16)
                    nc.vector.tensor_tensor(msg[:, :], bank[2][:, 0:C], rows_x[:, :],
                                            ALU.add).then_inc(s_msg, 1)
                    dve.wait_ge(s_msg, 2 * t + 1)
                    nc.vector.tensor_scalar(msg[:, :], msg[:, :], 0.0, None,
                                            ALU.max).then_inc(s_msg, 1)
                    dve.wait_ge(s_sum, t + 1)
                    dve.wait_ge(s_rows, 16 * t + 16)
                    nc.vector.tensor_tensor(rows_s[:, :], bank[3][:, 0:C], rows_s[:, :],
                                            ALU.add).then_inc(s_new, 1)
                dve.sem_inc(s_placed, 1)
                with dve.Fori(0, BLOCKS) as n:
                    dve.wait_ge(s_blockT, n + 1)
                    nc.vector.tensor_copy(aggT[:, :, bass.ds(n * P, P)],
                                          bank[0][:, 0:C].rearrange("p (c n) -> p c n", n=P)
                                          ).then_inc(s_placed, 1)

        @block.tensor
        def _(pe):
            with pe.If(flag(pe) > 0):
                pe.wait_ge(s_we, 1)
                with pe.Fori(0, TILES) as t:
                    pe.wait_ge(s_dst, t + 1)
                    nc.tensor.transpose(bank[1][:, 0:P], dst_f[:, 0:1].to_broadcast([P, P]),
                                        ident[:, :])
                    nc.tensor.transpose(bank[0][0:ED, 0:P], feat[:, :],
                                        ident[:, :]).then_inc(s_T, 1)
                    pe.wait_ge(s_featT, t + 1)
                    nc.tensor.matmul(bank[2][:, 0:C], featT[:, :], we[:, :], start=True,
                                     stop=True).then_inc(s_prod, 1)
                    pe.wait_ge(s_msg, 2 * t + 2)
                    nc.tensor.matmul(bank[3][:, 0:C], same[:, :], msg[:, :], start=True,
                                     stop=True).then_inc(s_sum, 1)
                with pe.Fori(0, BLOCKS) as n:
                    pe.wait_ge(s_block, 16 * n + 16)
                    pe.wait_ge(s_placed, n + 1)
                    for c in range(CC):
                        ins = nc.tensor.transpose(bank[0][:, c * P:(c + 1) * P],
                                                  block_rows[:, c * P:(c + 1) * P], ident[:, :])
                    ins.then_inc(s_blockT, 1)


def nodes(nc, k):
    aggT, ident, vecT, bank = k.aggT, k.ident, k.vecT, k.bank
    s_ = k.s12
    NT = CH // P
    with ExitStack() as ctx:
        def sb(name, shape, dt=fp32):
            return ctx.enter_context(nc.sbuf_tensor(name, shape, dt))

        def sem(name):
            return ctx.enter_context(nc.semaphore(name))

        th, tl = sb("th", [P, CC, CH], f32r), sb("tl", [P, CC, CH], f32r)
        h1 = sb("h1", [P, CC, CH])
        h1h, h1l = sb("h1h", [P, CC, CH], f32r), sb("h1l", [P, CC, CH], f32r)
        part, xT, t = (sb(n, [P, CC, CH]) for n in ("part2", "xT2", "t"))
        o = sb("o", [P, CC, CH])
        oh, ol = sb("oh2", [P, CC, CH], f32r), sb("ol2", [P, CC, CH], f32r)
        z = sb("z", [P, CC, CH])
        h2 = sb("h2", [P, 2, CH])
        h2h, h2l = sb("h2h", [P, 4, CH], f32r), sb("h2l", [P, 4, CH], f32r)
        xn = sb("xn2", [P, NT, C])
        r, y = sb("r", [P, NT, C]), sb("y", [P, NT, C])
        stats, mv = sb("stats", [P, NT, 6]), sb("mv", [P, NT, 2])
        sd, rstd = sb("sd", [P, NT]), sb("rstd", [P, NT])
        ve, fix = sb("ve", [P, NT]), sb("fix", [P, NT])

        s_part, s_x, s_out = sem("s_part_loaded"), sem("s_x_loaded2"), sem("s_stored")
        s_xT, s_u, s_t = sem("s_xT_loaded"), sem("s_part_completed"), sem("s_t_made")
        s_th, s_tl = sem("s_t_high"), sem("s_t_low")
        s_w1, s_h1h, s_h1l = sem("s_w1"), sem("s_h1_high"), sem("s_h1_low")
        s_w2, s_o, s_z, s_oh, s_ol = (sem(n) for n in ("s_w2", "s_out_made", "s_z", "s_out_high",
                                                       "s_out_low"))
        s_m1, s_h2h, s_h2l = sem("s_m1"), sem("s_h2_high"), sem("s_h2_low")
        s_m2, s_r, s_st, s_mv, s_sd, s_rs, s_y, s_chain = (sem(n) for n in (
            "s_m2", "s_row", "s_stats", "s_variance", "s_deviation", "s_rstd", "s_y",
            "s_norm_chain"))
        s_turn = sem("s_turn")
        block = ctx.enter_context(nc.Block())

        def since(c, first):
            return c >= first if isinstance(c, int) else True

        def run(body):
            def steps(engine):
                for c in range(3):
                    body(engine, c, True, c >= 1, c >= 2)
                with engine.Fori(3, NCH - 1) as c:
                    body(engine, c, True, True, True)
                body(engine, NCH - 1, True, True, True)
                body(engine, NCH, False, True, True)
                body(engine, NCH + 1, False, False, True)
            return steps

        x_v = k.x.rearrange("(c t p) f -> c p t f", t=NT, p=P)
        out_v = k.out.rearrange("(c t p) f -> c p t f", t=NT, p=P)

        @block.sync
        def _(sp):
            def load(to, of, c, loaded):
                for two in range(2):
                    sp.dma_start(to[:, :, two * NB:(two + 1) * NB],
                                 of[bass.ds(2 * c + two, 1), :, :, :].rearrange(
                                     "a p b n -> (a p) b n")).then_inc(loaded, 16)

            load(xT, k.xT_dram, 0, s_xT)

            def body(sp, c, front, back, norm):
                if front:
                    if since(c, 1):
                        sp.wait_ge(s_o, 2 * c)
                    load(part, k.part_dram, c, s_part)
                if back:
                    if since(c, 2):
                        sp.wait_ge(s_r, 2 * (c - 1))
                    sp.dma_start(xn[:, :, :], x_v[bass.ds(c - 1, 1), :, :, :].rearrange(
                        "a p t f -> (a p) t f")).then_inc(s_x, 16)
                if front and not (isinstance(c, int) and c == NCH - 1):
                    sp.wait_ge(s_u, c + 1)
                    load(xT, k.xT_dram, c + 1, s_xT)
                if norm:
                    sp.wait_ge(s_y, c - 1)
                    sp.dma_start(out_v[bass.ds(c - 2, 1), :, :, :].rearrange(
                        "a p t f -> (a p) t f"), y[:, :, :]).then_inc(s_out, 16)
            run(body)(sp)
            sp.wait_ge(s_out, 16 * NCH)

        @block.scalar
        def _(act):
            def high_of_t(c):
                act.wait_ge(s_t, c + 1)
                nc.scalar.copy(th[:, :, :], t[:, :, :]).then_inc(s_th, 1)

            high_of_t(0)

            def body(act, c, front, back, norm):
                if front:
                    for b in range(CC):
                        bias = vecT[:, V_B1 + b:V_B1 + b + 1]
                        act.wait_ge(s_w1, 2 * c + b + 1)
                        if since(c, 1):
                            act.wait_ge(s_h1l, 2 * c)
                            act.wait_ge(s_w2, 2 * c)
                        nc.scalar.activation(h1[:, b, :], bank[b][:, :], ACT.Relu, bias=bias)
                        nc.scalar.activation(h1h[:, b, :], bank[b][:, :], ACT.Relu,
                                             bias=bias).then_inc(s_h1h, 1)
                if norm:
                    act.wait_ge(s_mv, c - 1)
                    nc.scalar.activation(sd[:, :], ve[:, :], ACT.Sqrt).then_inc(s_sd, 1)
                if back:
                    for b in range(4):
                        bias = vecT[:, V_MB1 + b:V_MB1 + b + 1]
                        n = 4 * (c - 1) + b
                        act.wait_ge(s_m1, n + 1)
                        if since(c, 2) or b >= 2:
                            act.wait_ge(s_h2l, n - 1)
                        if since(c, 2):
                            act.wait_ge(s_m2, 2 * (c - 1))
                        nc.scalar.activation(h2[:, b % 2, :], bank[2 + b][:, :], ACT.Relu,
                                             bias=bias)
                        nc.scalar.activation(h2h[:, b, :], bank[2 + b][:, :], ACT.Relu,
                                             bias=bias).then_inc(s_h2h, 1)
                if front:
                    for b in range(CC):
                        act.wait_ge(s_o, 2 * c + b + 1)
                        if since(c, 1):
                            act.wait_ge(s_m1, 4 * c)
                        nc.scalar.copy(oh[:, b, :], o[:, b, :]).then_inc(s_oh, 1)
                    if not (isinstance(c, int) and c == NCH - 1):
                        act.wait_ge(s_w1, 2 * c + 2)
                        high_of_t(c + 1)
                    if since(c, 1):
                        act.wait_ge(s_m2, 2 * c)
                    for b in range(CC):
                        nc.scalar.activation(z[:, b, :], o[:, b, :], ACT.Identity,
                                             bias=k.c3[:, b:b + 1],
                                             scale=s_[:, 4 + b:5 + b]).then_inc(s_z, 1)
            run(body)(act)

        @block.vector
        def _(dve):
            def make_t(c):
                dve.wait_ge(s_xT, 32 * (c + 1))
                nc.vector.tensor_tensor(t[:, :, :], aggT[:, :, bass.ds(c * CH, CH)], xT[:, :, :],
                                        ALU.add).then_inc(s_t, 1)

            def low_of_t(c):
                dve.wait_ge(s_th, c + 1)
                nc.vector.tensor_tensor(tl[:, :, :], t[:, :, :], th[:, :, :].bitcast(fp32),
                                        ALU.subtract).then_inc(s_tl, 1)

            make_t(0)
            low_of_t(0)

            def body(dve, c, front, back, norm):
                if norm:
                    d = c - 2
                    dve.wait_ge(s_x, 16 * (c - 1))
                    for b in range(2):
                        dve.wait_ge(s_m2, 2 * d + b + 1)
                        if since(c, 3):
                            dve.wait_ge(s_y, d)
                        nc.vector.tensor_tensor(
                            r[:, 2 * b:2 * b + 2, :],
                            bank[6 + b][:, :].rearrange("p (t f) -> p t f", f=C),
                            xn[:, 2 * b:2 * b + 2, :], ALU.add).then_inc(s_r, 1)
                        dve.wait_ge(s_r, 2 * d + b + 1)
                        for t in (2 * b, 2 * b + 1):
                            ins = nc.vector.bn_stats(stats[:, t, :], r[:, t, :])
                        ins.then_inc(s_st, 1)
                    dve.wait_ge(s_st, 2 * d + 2)
                    dve.sem_inc(s_turn, 1)
                    for t in range(NT):
                        ins = nc.vector.bn_aggr(mv[:, t, :], stats[:, t, :])
                    ins.then_inc(s_chain, 1)
                    dve.wait_ge(s_chain, 5 * d + 1)
                    nc.vector.tensor_scalar(ve[:, :], mv[:, :, 1], LN_EPS, None,
                                            ALU.add).then_inc(s_mv, 1)
                if front:
                    for b in range(CC):
                        dve.wait_ge(s_h1h, 2 * c + b + 1)
                        nc.vector.tensor_tensor(h1l[:, b, :], h1[:, b, :],
                                                h1h[:, b, :].bitcast(fp32),
                                                ALU.subtract).then_inc(s_h1l, 1)
                if norm:
                    dve.wait_ge(s_sd, c - 1)
                    nc.vector.reciprocal(rstd[:, :], sd[:, :]).then_inc(s_chain, 1)
                    dve.wait_ge(s_chain, 5 * d + 2)
                    nc.vector.tensor_tensor(fix[:, :], rstd[:, :], rstd[:, :],
                                            ALU.mult).then_inc(s_chain, 1)
                    dve.wait_ge(s_chain, 5 * d + 3)
                    nc.vector.tensor_tensor(fix[:, :], fix[:, :], ve[:, :],
                                            ALU.mult).then_inc(s_chain, 1)
                    dve.wait_ge(s_chain, 5 * d + 4)
                    nc.vector.tensor_scalar(fix[:, :], fix[:, :], -0.5, 1.5, ALU.mult,
                                            ALU.add).then_inc(s_chain, 1)
                    dve.wait_ge(s_chain, 5 * d + 5)
                    nc.vector.tensor_tensor(rstd[:, :], rstd[:, :], fix[:, :],
                                            ALU.mult).then_inc(s_rs, 1)
                    dve.wait_ge(s_rs, c - 1)
                    if since(c, 3):
                        dve.wait_ge(s_out, 16 * d)
                    for t in range(NT):
                        ins = nc.vector.tensor_scalar(y[:, t, :], r[:, t, :], mv[:, t, 0:1],
                                                      rstd[:, t:t + 1], ALU.subtract, ALU.mult)
                    ins.then_inc(s_y, 1)
                if front:
                    dve.wait_ge(s_part, 32 * (c + 1))
                    for b in range(CC):
                        ins = nc.vector.scalar_tensor_tensor(part[:, b, :], xT[:, b, :],
                                                             s_[:, 6 + b:7 + b], part[:, b, :],
                                                             ALU.mult, ALU.add)
                    ins.then_inc(s_u, 1)
                if back:
                    for b in range(4):
                        dve.wait_ge(s_h2h, 4 * (c - 1) + b + 1)
                        nc.vector.tensor_tensor(h2l[:, b, :], h2[:, b % 2, :],
                                                h2h[:, b, :].bitcast(fp32),
                                                ALU.subtract).then_inc(s_h2l, 1)
                if front:
                    more = not (isinstance(c, int) and c == NCH - 1)
                    dve.wait_ge(s_u, c + 1)
                    for b in range(CC):
                        dve.wait_ge(s_w2, 2 * c + b + 1)
                        if since(c, 1):
                            dve.wait_ge(s_z, 2 * c)
                        nc.vector.scalar_tensor_tensor(o[:, b, :], bank[b][:, :], s_[:, b:b + 1],
                                                       part[:, b, :], ALU.mult,
                                                       ALU.add).then_inc(s_o, 1)
                    if more:
                        make_t(c + 1)
                    for b in range(CC):
                        dve.wait_ge(s_oh, 2 * c + b + 1)
                        nc.vector.tensor_tensor(ol[:, b, :], o[:, b, :],
                                                oh[:, b, :].bitcast(fp32),
                                                ALU.subtract).then_inc(s_ol, 1)
                    if more:
                        low_of_t(c + 1)
            run(body)(dve)

        @block.tensor
        def _(pe):
            def product(to, blocks, stationary, moving, more=False):
                terms = [(c, a, b) for c in range(blocks) for a, b in ((0, 0), (0, 1), (1, 0))]
                for n, (c, a, b) in enumerate(terms):
                    ins = nc.tensor.matmul(to, stationary[a](c), moving[b](c), start=n == 0,
                                           stop=not more and n == len(terms) - 1)
                return ins

            def body(pe, c, front, back, norm):
                if front:
                    pe.wait_ge(s_tl, c + 1)
                    if since(c, 1):
                        pe.wait_ge(s_o, 2 * c)
                    for b in range(CC):
                        col = slice(b * P, (b + 1) * P)
                        product(bank[b][:, :], CC,
                                [lambda n: k.w1h[:, n, col], lambda n: k.w1l[:, n, col]],
                                [lambda n: th[:, n, :], lambda n: tl[:, n, :]]).then_inc(s_w1, 1)
                if back:
                    pe.wait_ge(s_ol, 2 * c)
                    for b in range(4):
                        col = slice(b * P, (b + 1) * P)
                        if since(c, 2):
                            pe.wait_ge(s_h2h, 4 * (c - 1))
                        product(bank[2 + b][:, :], CC,
                                [lambda n: k.m1h[:, n, col], lambda n: k.m1l[:, n, col]],
                                [lambda n: oh[:, n, :], lambda n: ol[:, n, :]]).then_inc(s_m1, 1)
                if front:
                    pe.wait_ge(s_h1l, 2 * c + 2)
                    for b in range(CC):
                        col = slice(b * P, (b + 1) * P)
                        product(bank[b][:, :], CC,
                                [lambda n: k.w2h[:, n, col], lambda n: k.w2l[:, n, col]],
                                [lambda n: h1h[:, n, :], lambda n: h1l[:, n, :]]).then_inc(s_w2, 1)
                if back:
                    pe.wait_ge(s_h2l, 4 * c)
                    pe.wait_ge(s_z, 2 * c)
                    if since(c, 2):
                        pe.wait_ge(s_r, 2 * (c - 1))
                    for t in range(NT):
                        row = slice(t * P, (t + 1) * P)
                        to = bank[6 + t // 2][:, (t % 2) * C:(t % 2 + 1) * C]
                        product(to, 4,
                                [lambda n: h2h[:, n, row], lambda n: h2l[:, n, row]],
                                [lambda n: k.m2h[:, n, :], lambda n: k.m2l[:, n, :]], more=True)
                        for n in range(CC):
                            ins = nc.tensor.matmul(to[:, n * P:(n + 1) * P], z[:, n, row],
                                                   ident[:, :], start=False, stop=n == CC - 1)
                        if t % 2:
                            ins.then_inc(s_m2, 1)
            run(body)(pe)


_INS = ["x", "src", "dst", "edge_attr_64"] + ["L0_gnn_" + n for n in (
    "w_e", "b_e", "w1", "b1", "w2", "b2", "bn1_g", "bn1_b", "in_w", "in_b", "out_w", "out_b",
    "bn2_g", "bn2_b", "m_w1", "m_b1", "m_w2", "m_b2", "bn3_g", "bn3_b")]


def kernel(**inputs):
    import numpy as _np
    import concourse.bacc as _bacc
    from concourse import mybir as _mybir
    from concourse.bass_utils import run_bass_kernel_spmd as _run

    nc = _bacc.Bacc("TRN2", target_bir_lowering=False, num_devices=1)
    arrays, args = {}, []
    for name in _INS:
        a = _np.ascontiguousarray(inputs[name])
        arrays[f"in_{name}_dram"] = a
        args.append(nc.dram_tensor(f"in_{name}_dram", a.shape, _mybir.dt.from_np(a.dtype),
                                   kind="ExternalInput").ap())
    out = nc.dram_tensor("out_0_dram", (N, C), fp32, kind="ExternalOutput").ap()
    gnn_layer(nc, *args, out)
    r = _run(nc, [arrays], core_ids=[0])
    return r.results[0]["out_0_dram"]
```
